# Optimizing a Trainium2 kernel written in Bass

```python
import numpy as np
import jax
import jax.numpy as jnp

def _softmax(x, axis=-1):
    return jax.nn.softmax(x, axis=axis)
def _gelu(x):
    return jax.nn.gelu(x, approximate=True)
def _silu(x):
    return jax.nn.silu(x)
def _sigmoid(x):
    return jax.nn.sigmoid(x)
def _layernorm(x, axis=-1, eps=1e-5):
    m = jnp.mean(x, axis=axis, keepdims=True)
    v = jnp.var(x, axis=axis, keepdims=True)
    return (x - m) / jnp.sqrt(v + eps)
def _scatter_add(tgt, idx, src, axis=0):
    return tgt.at[idx].add(src)
def _segment_sum(src, seg, n):
    return jax.ops.segment_sum(src, seg, n)

kernel_name = 'mk_conv_preact_d2_conv_nchw64_a7d649'

def setup_inputs(seed: int = 0):
    np.random.seed(seed)
    _w = jnp.asarray
    def _rec_inputs():
        import jax
        import jax.numpy as jnp
        _gk = jax.random.key(seed)
        x = -0.0003929 + 0.9999 * jax.random.normal(jax.random.fold_in(_gk, 1), (16, 64, 128, 128), jnp.float32)
        return x
    x = _rec_inputs()
    def _L0_conv_setup():
        import jax, jax.numpy as jnp
        from jax import lax
        import numpy as np
        TRUNC = 16
        key = jax.random.key(seed)
        k1, k2, k3 = jax.random.split(key, 3)
        B, C_in, C_out, H, W, K = (16, 64, 64, 128, 128, 3)
        x = jax.random.normal(k1, (B, C_in, H, W), dtype=jnp.float32)
        conv_w = 0.05 * jax.random.normal(k2, (C_out, C_in, K), dtype=jnp.float32)
        conv_b = 0.05 * jax.random.normal(k3, (C_out,), dtype=jnp.float32)
        bias = jnp.zeros((1,), dtype=jnp.float32)
        return {'x': x, 'conv_w': conv_w, 'conv_b': conv_b, 'bias': bias}
    _L0_conv_all = _L0_conv_setup()
    _L0_conv_in = {k: v for k, v in _L0_conv_all.items() if k in ('conv_w', 'conv_b', 'bias', )}
    del _L0_conv_all

    def _L1_conv_setup():
        import math
        import jax, jax.numpy as jnp
        import numpy as np
        M_TILE = 8
        R_K = 3
        N = M_TILE + R_K - 1
        PAD = 1
        SCALE_BITS = 20

        def _rot_mats(n, inverse):
            sign = 1.0 if inverse else -1.0
            k = np.arange(n)[:, None]
            i = np.arange(n)[None, :]
            ang = sign * 2.0 * np.pi * k * i / n
            ang = (ang + np.pi) % (2.0 * np.pi) - np.pi
            neg = np.zeros((n, n), dtype=bool)
            hi = ang > np.pi / 2
            ang = np.where(hi, ang - np.pi, ang)
            neg |= hi
            lo = ang < -np.pi / 2
            ang = np.where(lo, ang + np.pi, ang)
            neg |= lo
            S = float(2 ** SCALE_BITS)
            lam = np.round(-np.tan(ang / 2.0) * S) / S
            gam = np.round(np.sin(ang) * S) / S
            s = np.where(neg, -1.0, 1.0)
            Mrr = s * (1.0 + lam * gam)
            Mri = s * (2.0 * lam + gam * lam * lam)
            Mir = s * gam
            Mii = s * (1.0 + gam * lam)
            f32 = lambda a: jnp.asarray(a, dtype=jnp.float32)
            return (f32(Mrr), f32(Mri), f32(Mir), f32(Mii))
        FWD_MATS = _rot_mats(N, inverse=False)
        INV_MATS = _rot_mats(N, inverse=True)

        def _t1d(xre, xim, mats, scale):
            Mrr, Mri, Mir, Mii = mats
            if xim is None:
                ore = xre @ Mrr.T
                oim = xre @ Mir.T
            else:
                ore = xre @ Mrr.T + xim @ Mri.T
                oim = xre @ Mir.T + xim @ Mii.T
            if scale != 1.0:
                ore = ore * scale
                oim = oim * scale
            return (ore, oim)

        def _t2d(xre, xim, mats, scale):
            re, im = _t1d(xre, xim, mats, scale)
            re = jnp.swapaxes(re, -1, -2)
            im = jnp.swapaxes(im, -1, -2)
            re, im = _t1d(re, im, mats, scale)
            return (jnp.swapaxes(re, -1, -2), jnp.swapaxes(im, -1, -2))

        def _forward(x, weight_re, weight_im):
            B, C, H, W = x.shape
            O = weight_re.shape[0]
            xp = jnp.pad(x, ((0, 0), (0, 0), (PAD, PAD), (PAD, PAD)))
            Hp, Wp = (H + 2 * PAD, W + 2 * PAD)
            th = max(1, math.ceil((Hp - N) / M_TILE) + 1)
            tw = max(1, math.ceil((Wp - N) / M_TILE) + 1)
            Hq = (th - 1) * M_TILE + N
            Wq = (tw - 1) * M_TILE + N
            if Hq > Hp or Wq > Wp:
                xp = jnp.pad(xp, ((0, 0), (0, 0), (0, Hq - Hp), (0, Wq - Wp)))
            r_idx = (np.arange(th) * M_TILE)[:, None] + np.arange(N)
            c_idx = (np.arange(tw) * M_TILE)[:, None] + np.arange(N)
            tiles = xp[:, :, r_idx[:, None, :, None], c_idx[None, :, None, :]]
            L = th * tw
            tiles = tiles.transpose(0, 2, 3, 1, 4, 5).reshape(B, L, C, N, N)
            Xre, Xim = _t2d(tiles, None, FWD_MATS, 1.0)
            Yre = jnp.einsum('blixy,oixy->bloxy', Xre, weight_re) - jnp.einsum('blixy,oixy->bloxy', Xim, weight_im)
            Yim = jnp.einsum('blixy,oixy->bloxy', Xre, weight_im) + jnp.einsum('blixy,oixy->bloxy', Xim, weight_re)
            ore, _ = _t2d(Yre, Yim, INV_MATS, 1.0 / N)
            start = (R_K - 1) // 2
            out = ore[..., start:start + M_TILE, start:start + M_TILE]
            out = out.reshape(B, th, tw, O, M_TILE, M_TILE)
            out = out.transpose(0, 3, 1, 4, 2, 5).reshape(B, O, th * M_TILE, tw * M_TILE)
            return out[:, :, :H, :W]
        key = jax.random.key(seed)
        k1, k2, k3 = jax.random.split(key, 3)
        B, C, O, H, W = (8, 64, 64, 224, 224)
        x = jax.random.normal(k1, (B, C, H, W), dtype=jnp.float32)
        weight_re = jax.random.normal(k2, (O, C, N, N), dtype=jnp.float32)
        weight_im = jax.random.normal(k3, (O, C, N, N), dtype=jnp.float32)
        return {'x': x, 'weight_re': weight_re, 'weight_im': weight_im}
    _L1_conv_all = _L1_conv_setup()
    _L1_conv_in = {k: v for k, v in _L1_conv_all.items() if k in ('weight_re', 'weight_im', )}
    del _L1_conv_all

    return {
        "x": x,
        "L0_conv_conv_w": _L0_conv_in["conv_w"],
        "L0_conv_conv_b": _L0_conv_in["conv_b"],
        "L0_conv_bias": _L0_conv_in["bias"],
        "L1_conv_weight_re": _L1_conv_in["weight_re"],
        "L1_conv_weight_im": _L1_conv_in["weight_im"],
    }

def reference(x, L0_conv_conv_w, L0_conv_conv_b, L0_conv_bias, L1_conv_weight_re, L1_conv_weight_im):
    import jax
    import jax.numpy as jnp
    def _L0_conv_ref(x, conv_w, conv_b, bias):
        import jax, jax.numpy as jnp
        from jax import lax
        import numpy as np
        TRUNC = 16
        B, C, H, W = x.shape
        K = conv_w.shape[-1]
        w2d = jnp.broadcast_to(conv_w[..., None], conv_w.shape + (K,))
        pad = K // 2
        conv_out = lax.conv_general_dilated(x, w2d, window_strides=(1, 1), padding=[(pad, pad), (pad, pad)], dimension_numbers=('NCHW', 'OIHW', 'NCHW'))
        conv_out = conv_out + conv_b[None, :, None, None]
        x_fft = jnp.fft.fftn(x, axes=(2, 3))[..., :TRUNC, :TRUNC]
        w_pad = jnp.pad(w2d, ((0, 0), (0, 0), (0, H - K), (0, W - K)))
        k_fft = jnp.fft.fftn(w_pad, axes=(2, 3))[..., :TRUNC, :TRUNC]
        out_fft = jnp.einsum('bcxy,kcxy->bkxy', x_fft, k_fft)
        out = jnp.fft.ifftn(out_fft, s=(H, W), axes=(2, 3)).real
        return out + conv_out + bias

    def _L1_conv_ref(x, weight_re, weight_im):
        import math
        import jax, jax.numpy as jnp
        import numpy as np
        M_TILE = 8
        R_K = 3
        N = M_TILE + R_K - 1
        PAD = 1
        SCALE_BITS = 20

        def _rot_mats(n, inverse):
            sign = 1.0 if inverse else -1.0
            k = np.arange(n)[:, None]
            i = np.arange(n)[None, :]
            ang = sign * 2.0 * np.pi * k * i / n
            ang = (ang + np.pi) % (2.0 * np.pi) - np.pi
            neg = np.zeros((n, n), dtype=bool)
            hi = ang > np.pi / 2
            ang = np.where(hi, ang - np.pi, ang)
            neg |= hi
            lo = ang < -np.pi / 2
            ang = np.where(lo, ang + np.pi, ang)
            neg |= lo
            S = float(2 ** SCALE_BITS)
            lam = np.round(-np.tan(ang / 2.0) * S) / S
            gam = np.round(np.sin(ang) * S) / S
            s = np.where(neg, -1.0, 1.0)
            Mrr = s * (1.0 + lam * gam)
            Mri = s * (2.0 * lam + gam * lam * lam)
            Mir = s * gam
            Mii = s * (1.0 + gam * lam)
            f32 = lambda a: jnp.asarray(a, dtype=jnp.float32)
            return (f32(Mrr), f32(Mri), f32(Mir), f32(Mii))
        FWD_MATS = _rot_mats(N, inverse=False)
        INV_MATS = _rot_mats(N, inverse=True)

        def _t1d(xre, xim, mats, scale):
            Mrr, Mri, Mir, Mii = mats
            if xim is None:
                ore = xre @ Mrr.T
                oim = xre @ Mir.T
            else:
                ore = xre @ Mrr.T + xim @ Mri.T
                oim = xre @ Mir.T + xim @ Mii.T
            if scale != 1.0:
                ore = ore * scale
                oim = oim * scale
            return (ore, oim)

        def _t2d(xre, xim, mats, scale):
            re, im = _t1d(xre, xim, mats, scale)
            re = jnp.swapaxes(re, -1, -2)
            im = jnp.swapaxes(im, -1, -2)
            re, im = _t1d(re, im, mats, scale)
            return (jnp.swapaxes(re, -1, -2), jnp.swapaxes(im, -1, -2))

        def _forward(x, weight_re, weight_im):
            B, C, H, W = x.shape
            O = weight_re.shape[0]
            xp = jnp.pad(x, ((0, 0), (0, 0), (PAD, PAD), (PAD, PAD)))
            Hp, Wp = (H + 2 * PAD, W + 2 * PAD)
            th = max(1, math.ceil((Hp - N) / M_TILE) + 1)
            tw = max(1, math.ceil((Wp - N) / M_TILE) + 1)
            Hq = (th - 1) * M_TILE + N
            Wq = (tw - 1) * M_TILE + N
            if Hq > Hp or Wq > Wp:
                xp = jnp.pad(xp, ((0, 0), (0, 0), (0, Hq - Hp), (0, Wq - Wp)))
            r_idx = (np.arange(th) * M_TILE)[:, None] + np.arange(N)
            c_idx = (np.arange(tw) * M_TILE)[:, None] + np.arange(N)
            tiles = xp[:, :, r_idx[:, None, :, None], c_idx[None, :, None, :]]
            L = th * tw
            tiles = tiles.transpose(0, 2, 3, 1, 4, 5).reshape(B, L, C, N, N)
            Xre, Xim = _t2d(tiles, None, FWD_MATS, 1.0)
            Yre = jnp.einsum('blixy,oixy->bloxy', Xre, weight_re) - jnp.einsum('blixy,oixy->bloxy', Xim, weight_im)
            Yim = jnp.einsum('blixy,oixy->bloxy', Xre, weight_im) + jnp.einsum('blixy,oixy->bloxy', Xim, weight_re)
            ore, _ = _t2d(Yre, Yim, INV_MATS, 1.0 / N)
            start = (R_K - 1) // 2
            out = ore[..., start:start + M_TILE, start:start + M_TILE]
            out = out.reshape(B, th, tw, O, M_TILE, M_TILE)
            out = out.transpose(0, 3, 1, 4, 2, 5).reshape(B, O, th * M_TILE, tw * M_TILE)
            return out[:, :, :H, :W]
        return _forward(x, weight_re, weight_im)

    def _gn(v, G=32, eps=1e-5):
        B_, C_, H_, W_ = v.shape
        g = v.reshape(B_, G, C_ // G, H_, W_)
        m = jnp.mean(g, axis=(2, 3, 4), keepdims=True)
        s = jnp.var(g, axis=(2, 3, 4), keepdims=True)
        return ((g - m) / jnp.sqrt(s + eps)).reshape(v.shape)

    def _ln_c(v, eps=1e-6):
        m = jnp.mean(v, axis=1, keepdims=True)
        s = jnp.var(v, axis=1, keepdims=True)
        return (v - m) / jnp.sqrt(s + eps)

    def _ln_t(v, eps=1e-5):
        m = jnp.mean(v, axis=-1, keepdims=True)
        s = jnp.var(v, axis=-1, keepdims=True)
        return (v - m) / jnp.sqrt(s + eps)

    def _to_tokens(v):
        B_, C_, H_, W_ = v.shape
        return v.reshape(B_, C_, H_ * W_).transpose(0, 2, 1)
    def _from_tokens(t, like):
        B_, C_, H_, W_ = like.shape
        return t.transpose(0, 2, 1).reshape(B_, C_, H_, W_)

    x = x + _L0_conv_ref(_gn(x), L0_conv_conv_w, L0_conv_conv_b, L0_conv_bias)
    x = x + _L1_conv_ref(_gn(x), L1_conv_weight_re, L1_conv_weight_im)
    return x


_drawn_inputs = setup_inputs


def setup_inputs(seed=0):
    import zlib

    import numpy as np

    out = dict(_drawn_inputs(seed))
    spreads = {}
    factors = {'L0_conv_conv_b': 2.822}
    for name, (base, spread) in spreads.items():
        noise = np.random.default_rng([zlib.crc32(name.encode()), seed]).standard_normal(out[name].shape)
        drawn = base * np.exp(spread * noise) if base else spread * noise
        out[name] = jnp.asarray(drawn.astype(out[name].dtype))
    for name, factor in factors.items():
        out[name] = (out[name] * factor).astype(out[name].dtype)
    return out
```

```python
import math

import numpy as np
import concourse.bass as bass
from concourse import mybir
from contextlib import ExitStack

C, H, W = 64, 128, 128
P = 128
GROUPS = 32
EPS = 1e-5
K0 = 3
TRUNC = 16
M_TILE, N_FREQ = 8, 10
TILES = H // M_TILE
PX = N_FREQ * N_FREQ
SLOTS = PX // 2

HALF = H // 2
ROWPAIRS = H // 2
BLOCKS = ROWPAIRS + 1
GCHUNK = 4
GCHUNKS = -(-BLOCKS // GCHUNK)
CONV_FILLS = ROWPAIRS // 4
PAIRS = TILES * TILES // 2
GRP = 2
T1_FILLS = PAIRS // GRP // 4
FW_FILLS = T1_FILLS // 2
FQ_FILLS = -(-SLOTS // 4)
T2_FILLS = C // 4
IN_FILLS = PAIRS // GRP // 8
INV_N = 96


def transform_matrices(inverse):
    n, sign = N_FREQ, 1.0 if inverse else -1.0
    k = np.arange(n)[:, None]
    i = np.arange(n)[None, :]
    ang = sign * 2.0 * np.pi * k * i / n
    ang = (ang + np.pi) % (2.0 * np.pi) - np.pi
    neg = np.zeros((n, n), dtype=bool)
    hi = ang > np.pi / 2
    ang = np.where(hi, ang - np.pi, ang)
    neg |= hi
    lo = ang < -np.pi / 2
    ang = np.where(lo, ang + np.pi, ang)
    neg |= lo
    size = float(2 ** 20)
    lam = np.round(-np.tan(ang / 2.0) * size) / size
    gam = np.round(np.sin(ang) * size) / size
    s = np.where(neg, -1.0, 1.0)
    out = (s * (1.0 + lam * gam), s * (2.0 * lam + gam * lam * lam), s * gam, s * (1.0 + gam * lam))
    return [m.astype(np.float32).astype(np.float64) for m in out]


def frequency_slots():
    slots, seen = [], set()
    for a in range(N_FREQ):
        for b in range(N_FREQ):
            partner = ((-a) % N_FREQ, (-b) % N_FREQ)
            if (a, b) != partner and partner not in seen:
                seen.add((a, b))
                slots.append(((a, b), (a, b), True))
    h = N_FREQ // 2
    slots.append(((0, 0), (0, h), False))
    slots.append(((h, 0), (h, h), False))
    return slots


def constants():
    f32 = np.float32
    out = {}
    out["ident"] = np.eye(P, dtype=f32)
    out["ident16"] = np.eye(P, dtype=np.float16)
    grp = (np.arange(P) % C) // (C // GROUPS)
    out["gmean"] = (grp[:, None] == grp[None, :]).astype(f32) / (2 * C // GROUPS)
    rr, ri, ir, ii = transform_matrices(False)
    re = np.einsum("bj,ai->ijab", rr, rr) + np.einsum("bj,ai->ijab", ir, ri)
    im = np.einsum("bj,ai->ijab", rr, ir) + np.einsum("bj,ai->ijab", ir, ii)
    fwd = np.zeros((P, 2, SLOTS))
    slots = frequency_slots()
    for n, (k, l, cplx) in enumerate(slots):
        fwd[:PX, 0, n] = re[:, :, k[0], k[1]].reshape(-1)
        fwd[:PX, 1, n] = (im if cplx else re)[:, :, l[0], l[1]].reshape(-1)
    out["fwd"] = fwd.reshape(P, PX).astype(f32)
    rr, ri, ir, ii = transform_matrices(True)
    sc = 1.0 / N_FREQ ** 2
    are = (np.einsum("jb,ia->abij", rr, rr) + np.einsum("jb,ia->abij", ir, ri)) * sc
    aim = (np.einsum("jb,ia->abij", ri, rr) + np.einsum("jb,ia->abij", ii, ri)) * sc
    inv = np.zeros((P, INV_N))
    for n, (k, l, cplx) in enumerate(slots):
        a = are[k[0], k[1], 1:1 + M_TILE, 1:1 + M_TILE].reshape(-1)
        b = (aim if cplx else are)[l[0], l[1], 1:1 + M_TILE, 1:1 + M_TILE].reshape(-1)
        half = 1.0 if cplx else 0.5
        inv[2 * n, :64], inv[2 * n + 1, :64] = half * a, half * b
    out["inv"] = inv.astype(f32)
    th = 2 * np.pi / H
    pos, kk = np.arange(H), np.arange(TRUNC)
    e = np.exp(-1j * th * pos[:, None] * kk[None, :])
    out["dft"] = np.stack([e.real, e.imag], -1).reshape(H, 2 * TRUNC).astype(f32)
    r = np.zeros((2, K0, TRUNC, 4, 2, 4, TRUNC, 2))
    for rih in range(2):
        for a in range(K0):
            for kx in range(TRUNC):
                for riw in range(2):
                    z = (1j ** (rih + riw)) * np.exp(-1j * th * a * kx)
                    for q in range(4):
                        r[rih, a, kx, q, riw, q, kx, 0] = z.real
                        r[rih, a, kx, q, riw, q, kx, 1] = z.imag
    out["taps"] = r.reshape(2 * K0, P, P).transpose(1, 0, 2).reshape(P, 2 * K0 * P).astype(f32)
    g = np.zeros((4, 2, 4, TRUNC, 2, H))
    ph = np.exp(1j * th * kk[:, None] * pos[None, :]) / (H * W)
    for q in range(4):
        g[q, 0, q, :, 0], g[q, 0, q, :, 1] = ph.real, -ph.imag
        g[q, 1, q, :, 0], g[q, 1, q, :, 1] = ph.imag, ph.real
    out["rows"] = g.reshape(8, P, H).transpose(1, 0, 2).reshape(P, 8 * H).astype(f32)
    box = sum(np.exp(-1j * th * b * kk) for b in range(K0))
    d = box[:, None] * np.exp(1j * th * kk[:, None] * pos[None, :])
    base = np.stack([d.real, -d.imag], 1).reshape(2 * TRUNC, W)
    hi = base.astype(np.float16)
    lo = (base - hi.astype(np.float64)).astype(np.float16)
    out["cols"] = np.concatenate([hi, lo, hi, lo], 0)
    return out


def conv_preact_kernel(nc, x, p_w, q_w, cw0, cw1, w_mix, conv_b, bias, c_ident, c_ident16, c_gmean, c_fwd,
                       c_inv, c_dft, c_taps, c_rows, c_cols, out):
    f32, f16 = mybir.dt.float32, mybir.dt.float16
    ALU = mybir.AluOpType
    ACT = mybir.ActivationFunctionType
    B = x.shape[0]
    U = 2
    TRIPS = B // U
    x_v = x.rearrange("(n u) c h w -> n u c h w", u=U)
    out_v = out.rearrange("(n u) c h w -> n u c h w", u=U)

    ctx = ExitStack()
    with ctx:
        def sb(name, shape, dt=f32):
            return ctx.enter_context(nc.sbuf_tensor(name, shape, dt))

        def sem(name):
            return ctx.enter_context(nc.semaphore(name))

        xr = [sb(f"xr{u}", [P, HALF, W]) for u in range(U)]
        xh = [sb(f"xh{r}", [P, 4, W]) for r in range(3)]
        g = [sb(f"g{r}", [P, GCHUNK, W + 2]) for r in range(2)]
        s_x = sb("s_x", [P, BLOCKS * W])
        s = s_x[:, :].rearrange("p (r w) -> p r w", w=W)
        spec = s_x[:, 0:SLOTS * P].rearrange("p (f t) -> p f t", t=P)
        tb = [s_x[:, SLOTS * P + 8 * PX * r:SLOTS * P + 8 * PX * (r + 1)] for r in range(2)]
        u2 = sb("u2", [P, (HALF + 2) * (W + 2)])
        xn = u2[:, :].rearrange("p (r w) -> p r w", w=W + 2)
        qt = u2[:, 0:C * P].rearrange("p (t h o) -> p t h o", h=2, o=C)
        ft = u2[:, 0:C * H // 2].bitcast(f16).rearrange("p (h o) -> p h o", o=C)
        wf = sb("wf", [P, SLOTS, P])
        u3 = sb("u3", [P, PX * C])
        yt = u3[:, :].rearrange("p (o k) -> p o k", k=PX)
        q_in = u3[:, :].rearrange("p (f o) -> p f o", o=P)
        a_t = u3[:, 0:2048].rearrange("p (j n) -> p j n", j=4)
        b_t = u3[:, 2048:4096].rearrange("p (k c) -> p k c", c=C)
        g16 = u3[:, 0:4096].bitcast(f16).rearrange("p (o v k) -> p o v k", v=4, k=2 * TRUNC)
        u_t = u3[:, 4096:4608].rearrange("p (q kx n) -> p q kx n", q=4, n=8)
        y_t = u3[:, 4608:6144].rearrange("p (q n) -> p q n", q=4)
        z_t = u3[:, 6144:6400]
        px = [sb(f"px{r}", [P, 4 * P]) for r in range(2)]
        ident, ident16 = sb("ident", [P, P]), sb("ident16", [P, P], f16)
        gmean, fwd, inv = sb("gmean", [P, P]), sb("fwd", [P, PX]), sb("inv", [P, INV_N])
        dft, taps, rows = sb("dft", [P, 2 * TRUNC]), sb("taps", [P, 2 * K0, P]), sb("rows", [P, 8, H])
        cols = sb("cols", [P, W], f16)
        w0, w1, wm = sb("w0", [P, P]), sb("w1", [P, P]), sb("wm", [P, 2 * K0 * C])
        brow, b1 = sb("brow", [1, C]), sb("b1", [1, 1])
        st = sb("st", [P, HALF // 4, 6])
        sm = [sb(f"sm{n}", [P, 12]) for n in range(2)]
        dcs = sb("dcs", [P, 1])
        carry = sb("carry", [P, 3])

        ps = [ctx.enter_context(nc.psum_tensor(f"ps{b}", [P, 512], f32)) for b in range(4)]
        pw = [ctx.enter_context(nc.psum_tensor(f"pw{b}", [P, 2, 512], f32)) for b in range(2)]
        wide = [pw[b // 2][:, b % 2, :] for b in range(4)]

        const_in, weight_in, weight_done = sem("const_in"), sem("weight_in"), sem("weight_done")
        pads_set = sem("pads_set")
        x_in = [sem(f"x_in{u}") for u in range(U)]
        xh_in = [sem(f"xh_in{r}") for r in range(3)]
        x_out = [sem(f"x_out{u}") for u in range(U)]
        xh_read = sem("xh_read")
        vec_step = sem("vec_step")
        stat_ready = sem("stat_ready")
        stat_mean = sem("stat_mean")
        v_ready, sd_ready = sem("v_ready"), sem("sd_ready")
        norm_ready = sem("norm_ready")
        pool_step = sem("pool_step")
        g_used = sem("g_used")
        a_done = sem("a_done")
        b_full, b_done = sem("b_full"), sem("b_done")
        uu_full, uu_done = sem("uu_full"), sem("uu_done")
        y_full, y_done = sem("y_full"), sem("y_done")
        z_full, z_done = sem("z_full"), sem("z_done")
        gg_full, hi_done, lo_done = sem("gg_full"), sem("hi_done"), sem("lo_done")
        dup_done = sem("dup_done")
        ft_full, ft_done = sem("ft_full"), sem("ft_done")
        conv_full, conv_done = sem("conv_full"), sem("conv_done")
        xn_mid, xn_ready = sem("xn_mid"), sem("xn_ready")
        t1_full, t1_done = sem("t1_full"), sem("t1_done")
        px_used, fw_even, fw_odd = sem("px_used"), sem("fw_even"), sem("fw_odd")
        fq_full, fq_done = sem("fq_full"), sem("fq_done")
        t2_full, t2_done = sem("t2_full"), sem("t2_done")
        in_full, in_done = sem("in_full"), sem("in_done")

        T1_ALL, FW_ALL, FQ_ALL = GRP * T1_FILLS, GRP * FW_FILLS, GRP * FQ_FILLS
        TB_ALL = T1_ALL // 2
        T2_ALL, IN_ALL = GRP * T2_FILLS, GRP * IN_FILLS
        XH_CHUNKS = C // 4

        def upto(it, u, per_image, k=0):
            return it * (U * per_image) + (u * per_image + k)

        def windows(row, col):
            return bass.AP(tensor=u2[:, :].tensor, offset=row * (W + 2) + col,
                           ap=[[(HALF + 2) * (W + 2), P], [M_TILE, 8], [W + 2, N_FREQ], [1, N_FREQ]])

        def apart(eng, h=0):
            if eng is nc.gpsimd:
                col = carry[C * h:C * h + 16, :]
                eng.tensor_tensor(col[:, 0:1], col[:, 2:3], col[:, 2:3], ALU.add)
            else:
                eng.tensor_copy(carry[:, 1:2], carry[:, 2:3])

        block = ctx.enter_context(nc.Block())

        @block.sync
        def _(sp):
            for dst, src in ((ident, c_ident), (gmean, c_gmean), (dft, c_dft), (ident16, c_ident16),
                             (cols, c_cols), (w0, cw0), (w1, cw1), (wm, w_mix), (fwd, c_fwd), (inv, c_inv),
                             (brow, conv_b), (b1, bias)):
                sp.dma_start(dst[:, :], src).then_inc(const_in, 16)
            sp.dma_start(taps[:, :, :], c_taps.rearrange("p (a m) -> p a m", m=P)).then_inc(const_in, 16)
            sp.dma_start(rows[:, :, :], c_rows.rearrange("p (a m) -> p a m", m=H)).then_inc(const_in, 16)
            sp.dma_start(wf[:, :, :], p_w).then_inc(weight_in, 16)
            sp.dma_start(q_in, q_w).then_inc(weight_in, 16)
            with sp.Fori(0, TRIPS) as it:
                for u in range(U):
                    sp.wait_ge(x_out[u], it * 32)
                    for h in range(2):
                        sp.dma_start(xr[u][C * h:C * h + C, :, :],
                                     x_v[it, u, :, HALF * h:HALF * h + HALF, :]).then_inc(x_in[u], 16)
                    for n in range(XH_CHUNKS):
                        m = u * XH_CHUNKS + n
                        if m >= 3:
                            sp.wait_ge(xh_read, upto(it, u, XH_CHUNKS, n - 2))
                        else:
                            sp.wait_ge(xh_read, it * (U * XH_CHUNKS))
                        sp.dma_start(xh[m % 3][:, :, :],
                                     x_v[it, u, 4 * n:4 * n + 4, :, :].rearrange("c h w -> h c w")
                                     ).then_inc(xh_in[m % 3], 16)

        def xh_count(it, m):
            per_trip = [len(range(r, U * XH_CHUNKS, 3)) for r in range(3)][m % 3]
            return it * (16 * per_trip) + 16 * (m // 3 + 1)

        def staggered(n):
            pieces = []
            for par in range(2):
                j, nb = 0, min(GCHUNK, BLOCKS - GCHUNK * n)
                while j < nb:
                    row = 2 * (GCHUNK * n + j) - 1 + par
                    cnt = 1
                    if 0 <= row < H:
                        while j + cnt < nb and row + 2 * cnt < H and (row + 2 * cnt) // HALF == row // HALF:
                            cnt += 1
                        pieces.append((par, j, cnt, row // HALF, row % HALF))
                    else:
                        pieces.append((par, j, cnt, None, None))
                    j += cnt
            return pieces

        POOL = sum(len(staggered(n)) for n in range(GCHUNKS)) + TB_ALL

        @block.gpsimd
        def _(pool):
            pool.wait_ge(pads_set, 1)
            with pool.Fori(0, TRIPS) as it:
                for u in range(U):
                    steps = [0]

                    def link(ins):
                        steps[0] += 1
                        ins.then_inc(pool_step, 1)
                        pool.wait_ge(pool_step, upto(it, u, POOL, steps[0]))

                    pool.wait_ge(norm_ready, upto(it, u, 2, 1))
                    for n in range(GCHUNKS):
                        k = u * GCHUNKS + n
                        if k >= 2:
                            pool.wait_ge(g_used, upto(it, u, GCHUNKS, n - 1))
                        else:
                            pool.wait_ge(g_used, it * (U * GCHUNKS))
                        for par, j, cnt, h, lr in staggered(n):
                            dst = g[k % 2][C * par:C * par + C, j:j + cnt, 1:W + 1]
                            apart(pool, par if h is None else h)
                            if h is None:
                                link(pool.memset(dst, 0.0))
                            else:
                                link(pool.tensor_scalar(dst, xr[u][C * h:C * h + C, lr:lr + 2 * cnt - 1:2, :],
                                                        sm[0][C * h:C * h + C, 6:7], sm[0][C * h:C * h + C, 8:9],
                                                        ALU.mult, ALU.add))
                    pool.wait_ge(norm_ready, upto(it, u, 2, 2))
                    pool.wait_ge(xn_ready, upto(it, u, 1, 1))
                    for n in range(TB_ALL):
                        if n >= 2:
                            pool.wait_ge(t1_full, upto(it, u, T1_ALL, 2 * (n - 1)))
                        apart(pool)
                        th, tw = 8 * n // TILES, 8 * n % TILES
                        dst = tb[n % 2].rearrange("p (t y x) -> p t y x", t=8, y=N_FREQ)
                        link(pool.tensor_copy(dst, windows(M_TILE * th, M_TILE * tw)))
                    assert steps[0] == POOL, steps[0]
                    for h in range(2):
                        pool.wait_ge(in_done, upto(it, u, IN_ALL, IN_ALL))
                        pool.dma_start(out_v[it, u, :, HALF * h:HALF * h + HALF, :],
                                       xr[u][C * h:C * h + C, :, :]).then_inc(x_out[u], 16)
            for u in range(U):
                pool.wait_ge(x_out[u], 32 * TRIPS)

        VEC = 2 + 5 + 6 + GCHUNKS + 1

        @block.vector
        def _(dve):
            dve.memset(u2[:, :], 0.0)
            for r in range(2):
                dve.memset(g[r][:, :, 0:1], 0.0)
                dve.memset(g[r][:, :, W + 1:W + 2], 0.0)
                dve.memset(px[r][96:P, :], 0.0)
            dve.memset(carry[:, :], 0.0)
            dve.memset(dcs[:, :], 0.0).then_inc(pads_set, 1)
            dve.wait_ge(pads_set, 1)
            dve.wait_ge(weight_in, 32)
            for lo_p, lo_c, op in ((0, 0, ALU.add), (C, C, ALU.add), (0, C, ALU.subtract), (C, 0, ALU.subtract)):
                blk = wf[lo_p:lo_p + C, :, lo_c:lo_c + C]
                ins = dve.tensor_tensor(blk, blk, q_in[lo_p:lo_p + C, :, lo_c:lo_c + C], op)
            ins.then_inc(weight_done, 1)
            dve.wait_ge(const_in, 16 * 14)
            dve.tensor_scalar(brow[:, :], brow[:, :], b1[:, :], float(H * W) / K0, ALU.add, ALU.mult).then_inc(weight_done, 1)
            dve.wait_ge(weight_done, 2)

            with dve.Fori(0, TRIPS) as it:
                for u in range(U):
                    chain = [0]

                    def link(ins):
                        chain[0] += 1
                        ins.then_inc(vec_step, 1)
                        dve.wait_ge(vec_step, upto(it, u, VEC, chain[0]))

                    def norm(n):
                        m = sm[n]
                        apart(dve)
                        dve.bn_aggr(m[:, 0:2], st[:, :, :]).then_inc(stat_ready, 1)
                        dve.wait_ge(stat_mean, upto(it, u, 4, 2 * n + 1))
                        link(dve.tensor_tensor(m[:, 2:3], m[:, 0:1], ps[1][:, 0:1], ALU.subtract))
                        dve.scalar_tensor_tensor(m[:, 3:4], m[:, 2:3], m[:, 2:3], m[:, 1:2],
                                                 ALU.mult, ALU.add).then_inc(stat_ready, 1)
                        dve.tensor_copy(m[:, 9:10], ps[1][:, 0:1])
                        dve.wait_ge(stat_mean, upto(it, u, 4, 2 * n + 2))
                        dve.tensor_scalar(m[:, 4:5], ps[0][:, 0:1], EPS, None, ALU.add).then_inc(v_ready, 1)
                        dve.wait_ge(sd_ready, upto(it, u, 2, n + 1))
                        link(dve.reciprocal(m[:, 6:7], m[:, 5:6]))
                        link(dve.tensor_scalar(m[:, 7:8], m[:, 6:7], m[:, 6:7], m[:, 4:5], ALU.mult, ALU.mult))
                        link(dve.tensor_scalar(m[:, 7:8], m[:, 7:8], -0.5, 1.5, ALU.mult, ALU.add))
                        link(dve.tensor_scalar(m[:, 6:7], m[:, 6:7], m[:, 7:8], None, ALU.mult))
                        return dve.tensor_scalar(m[:, 8:9], m[:, 9:10], m[:, 6:7], -1.0, ALU.mult, ALU.mult)

                    dve.wait_ge(x_in[u], it * 32 + 32)
                    for n in range(HALF // 4):
                        ins = dve.bn_stats(st[:, n, :], xr[u][:, 4 * n:4 * n + 4, :].rearrange("p r w -> p (r w)"))
                    link(ins)
                    link(norm(0))
                    dve.tensor_scalar(dcs[0:C, :], sm[0][0:C, 8:9], float(H * W), None, ALU.mult).then_inc(norm_ready, 1)

                    dve.wait_ge(fq_full, upto(it, u, FQ_ALL))
                    for n in range(GCHUNKS):
                        k = u * GCHUNKS + n
                        nb = min(GCHUNK, BLOCKS - GCHUNK * n)
                        dve.wait_ge(pool_step, upto(it, u, POOL, sum(len(staggered(m)) for m in range(n + 1))))
                        src, dst = g[k % 2], s[:, GCHUNK * n:GCHUNK * n + nb, :]
                        link(dve.tensor_tensor(dst, src[:, 0:nb, 0:W], src[:, 0:nb, 1:W + 1], ALU.add))
                        ins = dve.tensor_tensor(dst, dst, src[:, 0:nb, 2:W + 2], ALU.add)
                        ins.then_inc(g_used, 1)
                    for q in range(4):
                        dve.wait_ge(y_full, upto(it, u, 4, q + 1))
                        dve.tensor_copy(y_t[:, q, :], wide[q][:, 0:2 * K0 * C]).then_inc(y_done, 1)
                    dve.wait_ge(z_full, upto(it, u, 1, 1))
                    link(dve.tensor_copy(z_t, wide[0][:, 0:4 * C]))
                    dve.tensor_tensor(z_t[0:1, 0:C], z_t[0:1, 0:C], brow[:, :], ALU.add).then_inc(z_done, 1)
                    for q in range(4):
                        dve.wait_ge(hi_done, upto(it, u, 4, q + 1))
                        dst = g16.rearrange("p o v (kg q r) -> p v q r kg o", q=4, r=2)
                        src = wide[q].rearrange("p (r kg o) -> p r kg o", r=2, kg=4)
                        ins = dve.tensor_tensor(dst[:, 2, q, :], src, dst[:, 0, q, :], ALU.subtract)
                        ins.then_inc(lo_done, 1)
                    for n in range(8):
                        dve.wait_ge(ft_full, upto(it, u, 8, n + 1))
                        dve.tensor_copy(ft[:, :, 8 * n:8 * n + 8].rearrange("p h o -> p o h"),
                                        ps[2 + n % 2][:, :].bitcast(f16).rearrange("p (o h) -> p o h", h=H)
                                        ).then_inc(ft_done, 1)

                    for n in range(CONV_FILLS):
                        h, j = n % 2, n // 2
                        dve.wait_ge(conv_full, upto(it, u, CONV_FILLS, n + 1))
                        for par in range(2):
                            dst = xr[u][C * h:C * h + C, 8 * j + par:8 * j + 8:2, :]
                            ins = dve.tensor_tensor(dst, ps[n % 2][C * par:C * par + C, :].rearrange("p (r w) -> p r w", w=W),
                                                    dst, ALU.add)
                        ins.then_inc(conv_done, 1)
                        if h == 1:
                            dve.wait_ge(conv_done, upto(it, u, CONV_FILLS, n + 1))
                            for m in (2 * j, 2 * j + 1):
                                ins = dve.bn_stats(st[:, m, :], xr[u][:, 4 * m:4 * m + 4, :].rearrange("p r w -> p (r w)"))
                    link(ins)
                    dve.memset(xn[:, :, 0:1], 0.0)
                    dve.memset(xn[:, :, W + 1:W + 2], 0.0)
                    dve.memset(xn[0:C, 0:1, 1:W + 1], 0.0)
                    dve.memset(xn[C:P, HALF + 1:HALF + 2, 1:W + 1], 0.0)
                    norm(1).then_inc(norm_ready, 1)

                    def spectra(grp):
                        for n in range(0, FW_FILLS, 2):
                            k = grp * FW_FILLS + n
                            dve.wait_ge(px_used, upto(it, u, T1_ALL, 2 * (k + 1)))
                            if n == 0 and grp > 0:
                                dve.wait_ge(fq_full, upto(it, u, FQ_ALL, grp * FQ_FILLS))
                            for h in range(2):
                                src = pw[n % 2][C * h:C * h + C, :, 0:4 * PX].rearrange("p b (t v f) -> p v f b t", v=2, f=SLOTS)
                                for v in range(2):
                                    dst = spec[C * v:C * v + C, :, 64 * h + 8 * n:64 * h + 8 * n + 8].rearrange("p f (b t) -> p f b t", b=2)
                                    ins = dve.tensor_copy(dst, src[:, v])
                            ins.then_inc(fw_even, 1)

                    def result(grp):
                        for n in range(IN_FILLS):
                            k = grp * IN_FILLS + n
                            dve.wait_ge(in_full, upto(it, u, IN_ALL, k + 1))
                            th, tw = (grp * 64 + 8 * n) // TILES, (8 * n) % TILES
                            dst = xr[u][:, M_TILE * th:M_TILE * th + M_TILE, M_TILE * tw:M_TILE * tw + 64].rearrange(
                                "p y (t x) -> p t y x", t=8)
                            src = ps[n % 2][:, :].rearrange("p (t y x) -> p t y x", t=8, y=M_TILE)
                            dve.tensor_tensor(dst, src, dst, ALU.add).then_inc(in_done, 1)

                    spectra(0)
                    spectra(1)
                    result(0)
                    result(1)
                    assert chain[0] == VEC, chain[0]

        @block.scalar
        def _(act):
            act.wait_ge(pads_set, 1)
            with act.Fori(0, TRIPS) as it:
                for u in range(U):
                    def root(n):
                        act.wait_ge(v_ready, upto(it, u, 2, n + 1))
                        act.activation(sm[n][:, 5:6], sm[n][:, 4:5], ACT.Sqrt).then_inc(sd_ready, 1)

                    def norm_copy(dst, src, scale):
                        return act.activation(dst, src, ACT.Copy, scale=scale)

                    act.wait_ge(weight_done, 2)
                    act.wait_ge(t2_full, upto(it, u, T2_ALL))
                    for q in range(4):
                        act.wait_ge(xh_read, upto(it, u, XH_CHUNKS, 4 * (q + 1)))
                        act.copy(a_t[:, q, :], wide[q]).then_inc(a_done, 1)
                    for q in range(4):
                        act.wait_ge(b_full, upto(it, u, 4, q + 1))
                        dst = b_t[:, :, 16 * q:16 * q + 16].rearrange("p k (g cc) -> p cc g k", cc=4)
                        src = ps[2 + q % 2][:, :].rearrange("p (cc g k) -> p cc g k", cc=4, g=4)
                        act.copy(dst, src).then_inc(b_done, 1)
                    root(0)
                    act.wait_ge(norm_ready, upto(it, u, 2, 1))
                    act.wait_ge(uu_full, upto(it, u, 1, 1))
                    norm_copy(u_t, wide[0].rearrange("p (kx q n) -> p q kx n", q=4, n=8), sm[0][:, 6:7]).then_inc(uu_done, 1)
                    act.wait_ge(uu_done, upto(it, u, 2, 1))
                    act.activation(u_t[:, 0, 0, 0:1], u_t[:, 0, 0, 0:1], ACT.Identity, bias=dcs[:, :]).then_inc(uu_done, 1)
                    for q in range(4):
                        act.wait_ge(gg_full, upto(it, u, 4, q + 1))
                        dst = g16.rearrange("p o v (kg q r) -> p v q r kg o", q=4, r=2)
                        src = wide[q].rearrange("p (r kg o) -> p r kg o", r=2, kg=4)
                        act.copy(dst[:, 0, q, :], src)
                        act.copy(dst[:, 1, q, :], src).then_inc(hi_done, 1)
                    act.wait_ge(lo_done, upto(it, u, 4, 4))
                    act.copy(g16[:, :, 3, :], g16[:, :, 2, :]).then_inc(dup_done, 1)
                    root(1)
                    act.wait_ge(norm_ready, upto(it, u, 2, 2))
                    act.wait_ge(conv_full, upto(it, u, CONV_FILLS, CONV_FILLS))
                    act.activation(xn[:, 1:HALF + 1, 1:W + 1], xr[u][:, :, :], ACT.Identity,
                                   bias=sm[1][:, 8:9], scale=sm[1][:, 6:7]).then_inc(xn_mid, 1)
                    act.wait_ge(xn_mid, upto(it, u, 1, 1))
                    act.copy(xn[C:P, 0, 1:W + 1], xn[0:C, HALF, 1:W + 1])
                    act.copy(xn[0:C, HALF + 1, 1:W + 1], xn[C:P, 1, 1:W + 1]).then_inc(xn_ready, 1)

                    def pixels_and_spectra(grp):
                        for n in range(T1_FILLS + 1):
                            if n < T1_FILLS:
                                k = grp * T1_FILLS + n
                                act.wait_ge(t1_full, upto(it, u, T1_ALL, k + 1))
                                if k >= 2:
                                    act.wait_ge(px_used, upto(it, u, T1_ALL, k - 1))
                                act.copy(px[n % 2][0:PX, :], ps[2 + n % 2][0:PX, :]).then_inc(t1_done, 1)
                            if n >= 4 and n % 4 == 0:
                                m = n // 2 - 1
                                k = grp * FW_FILLS + m
                                act.wait_ge(px_used, upto(it, u, T1_ALL, 2 * (k + 1)))
                                if m == 1 and grp > 0:
                                    act.wait_ge(fq_full, upto(it, u, FQ_ALL, grp * FQ_FILLS))
                                for h in range(2):
                                    src = pw[m % 2][C * h:C * h + C, :, 0:4 * PX].rearrange("p b (t v f) -> p v f b t", v=2, f=SLOTS)
                                    for v in range(2):
                                        dst = spec[C * v:C * v + C, :, 64 * h + 8 * m:64 * h + 8 * m + 8].rearrange("p f (b t) -> p f b t", b=2)
                                        ins = act.copy(dst, src[:, v])
                                ins.then_inc(fw_odd, 1)

                    def products(grp):
                        for n in range(FQ_FILLS):
                            k = grp * FQ_FILLS + n
                            nf = min(4, SLOTS - 4 * n)
                            act.wait_ge(fq_full, upto(it, u, FQ_ALL, k + 1))
                            if n == 0 and grp > 0:
                                act.wait_ge(t2_full, upto(it, u, T2_ALL, grp * T2_FILLS))
                            src = wide[n % 4][:, 0:nf * P].rearrange("p (f v o) -> p f v o", f=nf, v=2)
                            dst = yt[:, :, 8 * n:8 * n + 2 * nf].rearrange("p o (f v) -> p f v o", v=2)
                            act.copy(dst, src).then_inc(fq_done, 1)

                    def transposed(grp):
                        for n in range(T2_FILLS):
                            k = grp * T2_FILLS + n
                            act.wait_ge(t2_full, upto(it, u, T2_ALL, k + 1))
                            if n == 0:
                                act.wait_ge(in_full if grp else t1_full,
                                            upto(it, u, IN_ALL, IN_FILLS) if grp else upto(it, u, T1_ALL, T1_ALL))
                            act.copy(qt[0:PX, :, :, 4 * n:4 * n + 4].rearrange("p t h o -> p o h t"),
                                     ps[2 + n % 2][0:PX, :].rearrange("p (o h t) -> p o h t", o=4, h=2)).then_inc(t2_done, 1)

                    pixels_and_spectra(0)
                    products(0)
                    pixels_and_spectra(1)
                    transposed(0)
                    products(1)
                    transposed(1)

        @block.tensor
        def _(pe):
            pe.wait_ge(const_in, 16 * 14)
            with pe.Fori(0, TRIPS) as it:
                for u in range(U):
                    def mean(n):
                        for j in range(2):
                            pe.wait_ge(stat_ready, upto(it, u, 4, 2 * n + j + 1))
                            pe.matmul(ps[1 - j][:, 0:1], gmean[:, :], sm[n][:, 0:1] if j == 0 else sm[n][:, 3:4],
                                      start=True, stop=True).then_inc(stat_mean, 1)

                    pe.wait_ge(fq_done, upto(it, u, FQ_ALL))
                    for n in range(XH_CHUNKS):
                        q, gq = n // 4, n % 4
                        m = u * XH_CHUNKS + n
                        pe.wait_ge(xh_in[m % 3], xh_count(it, m))
                        ins = pe.matmul(wide[q][32 * gq:32 * gq + 32, :], dft[:, :],
                                        xh[m % 3][:, :, :].rearrange("p c w -> p (c w)"), start=True, stop=True)
                        ins.then_inc(xh_read, 1)
                    pe.wait_ge(t2_done, upto(it, u, T2_ALL))
                    for q in range(4):
                        pe.wait_ge(a_done, upto(it, u, 4, q + 1))
                        if q >= 2:
                            pe.wait_ge(b_done, upto(it, u, 4, q - 1))
                        for cc in range(4):
                            ins = pe.transpose(ps[2 + q % 2][:, P * cc:P * cc + P], a_t[:, q, P * cc:P * cc + P], ident[:, :])
                        ins.then_inc(b_full, 1)
                    pe.wait_ge(in_done, upto(it, u, IN_ALL))
                    mean(0)
                    pe.wait_ge(b_done, upto(it, u, 4, 4))
                    for kx in range(TRUNC):
                        ins = pe.matmul(wide[0][:, 32 * kx:32 * kx + 32], b_t[:, 2 * kx:2 * kx + 2, :].rearrange("p k c -> p (k c)"),
                                        dft[:, :], start=True, stop=True)
                    ins.then_inc(uu_full, 1)
                    pe.wait_ge(uu_done, upto(it, u, 2, 2))
                    for q in range(4):
                        pe.matmul(wide[q][:, 0:2 * K0 * C], u_t[:, q, :, :].rearrange("p kx n -> p (kx n)"), wm[:, :],
                                  start=True, stop=True).then_inc(y_full, 1)
                    pe.wait_ge(y_done, upto(it, u, 4, 4))
                    for n in range(2 * K0):
                        ins = pe.matmul(wide[0][:, 0:4 * C].rearrange("p (q o) -> p q o", o=C), taps[:, n, :],
                                        y_t[:, :, C * n:C * n + C], start=(n == 0), stop=(n == 2 * K0 - 1))
                    ins.then_inc(z_full, 1)
                    pe.wait_ge(z_done, upto(it, u, 1, 1))
                    for q in range(4):
                        for r in range(2):
                            ins = pe.matmul(wide[q][:, 4 * C * r:4 * C * r + 4 * C], rows[:, 2 * q + r, :], z_t,
                                            start=True, stop=True)
                        ins.then_inc(gg_full, 1)
                    pe.wait_ge(dup_done, upto(it, u, 1, 1))
                    for n in range(8):
                        if n >= 2:
                            pe.wait_ge(ft_done, upto(it, u, 8, n - 1))
                        bank = ps[2 + n % 2][:, :].bitcast(f16)
                        for j in range(8):
                            ins = pe.transpose(bank[:, P * j:P * j + P], g16[:, 8 * n + j, :, :].rearrange("p v k -> p (v k)"),
                                               ident16[:, :])
                        ins.then_inc(ft_full, 1)
                    pe.wait_ge(ft_done, upto(it, u, 8, 8))
                    pe.wait_ge(g_used, upto(it, u, GCHUNKS, GCHUNKS))
                    for n in range(CONV_FILLS):
                        h, j = n % 2, n // 2
                        r = 32 * h + 4 * j
                        if n >= 2:
                            pe.wait_ge(conv_done, upto(it, u, CONV_FILLS, n - 1))
                        bank = ps[n % 2]
                        pe.matmul(bank[:, :], w0[:, :], s[:, r:r + 4, :].rearrange("p r w -> p (r w)"), start=True, stop=False)
                        pe.matmul(bank[:, :], w1[:, :], s[:, r + 1:r + 5, :].rearrange("p r w -> p (r w)"), start=False, stop=False)
                        for i in range(4):
                            ins = pe.matmul(bank[:, W * i:W * i + W],
                                            ft[:, 2 * (r + i):2 * (r + i) + 2, :].rearrange("p par o -> p (par o)"),
                                            cols[:, :], start=False, stop=(i == 3))
                        ins.then_inc(conv_full, 1)
                    pe.wait_ge(conv_done, upto(it, u, CONV_FILLS, CONV_FILLS))
                    mean(1)

                    def pixels_and_spectra(grp):
                        for n in range(T1_FILLS + 1):
                            if n < T1_FILLS:
                                k = grp * T1_FILLS + n
                                if k >= 2:
                                    pe.wait_ge(t1_done, upto(it, u, T1_ALL, k - 1))
                                pe.wait_ge(pool_step, upto(it, u, POOL, POOL - TB_ALL + k // 2 + 1))
                                for j in range(4):
                                    tile = tb[(k // 2) % 2][:, PX * (4 * (k % 2) + j):PX * (4 * (k % 2) + j) + PX]
                                    ins = pe.transpose(ps[2 + n % 2][0:PX, P * j:P * j + P], tile, ident[:, :])
                                ins.then_inc(t1_full, 1)
                            if n >= 1:
                                m = n - 1
                                k = grp * FW_FILLS + m // 2
                                if m % 2 == 0 and k >= 2:
                                    pe.wait_ge(fw_odd if k % 2 else fw_even, upto(it, u, FW_ALL // 2, k // 2))
                                if m == 0 and grp == 1:
                                    pe.wait_ge(fq_done, upto(it, u, FQ_ALL, FQ_FILLS))
                                pe.wait_ge(t1_done, upto(it, u, T1_ALL, grp * T1_FILLS + m + 1))
                                for j in range(4):
                                    ins = pe.matmul(pw[(m // 2) % 2][:, m % 2, PX * j:PX * j + PX],
                                                    px[m % 2][:, P * j:P * j + P], fwd[:, :], start=True, stop=True)
                                ins.then_inc(px_used, 1)

                    def products(grp):
                        pe.wait_ge(fw_even, upto(it, u, FW_ALL // 2, (grp + 1) * FW_FILLS // 2))
                        pe.wait_ge(fw_odd, upto(it, u, FW_ALL // 2, (grp + 1) * FW_FILLS // 2))
                        for n in range(FQ_FILLS):
                            k = grp * FQ_FILLS + n
                            if n >= 4:
                                pe.wait_ge(fq_done, upto(it, u, FQ_ALL, k - 3))
                            for j in range(min(4, SLOTS - 4 * n)):
                                ins = pe.matmul(wide[n % 4][:, P * j:P * j + P], spec[:, 4 * n + j, :], wf[:, 4 * n + j, :],
                                                start=True, stop=True)
                            ins.then_inc(fq_full, 1)

                    def transposed(grp):
                        pe.wait_ge(fq_done, upto(it, u, FQ_ALL, (grp + 1) * FQ_FILLS))
                        for n in range(T2_FILLS):
                            k = grp * T2_FILLS + n
                            if n >= 2:
                                pe.wait_ge(t2_done, upto(it, u, T2_ALL, k - 1))
                            elif n == 0:
                                pe.wait_ge(t1_done, upto(it, u, T1_ALL, T1_ALL))
                            for j in range(4):
                                ins = pe.transpose(ps[2 + n % 2][0:PX, P * j:P * j + P], yt[:, 4 * n + j, :], ident[:, :])
                            ins.then_inc(t2_full, 1)

                    def inverse(grp):
                        pe.wait_ge(t2_done, upto(it, u, T2_ALL, (grp + 1) * T2_FILLS))
                        for n in range(IN_FILLS):
                            k = grp * IN_FILLS + n
                            if k >= 2:
                                pe.wait_ge(in_done, upto(it, u, IN_ALL, k - 1))
                            for j in range(8):
                                t = 8 * n + j
                                nn = INV_N if j < 7 else 64
                                ins = pe.matmul(ps[n % 2][:, 64 * j:64 * j + nn],
                                                qt[:, t, :, :].rearrange("p h o -> p (h o)"),
                                                inv[:, 0:nn], start=True, stop=True)
                            ins.then_inc(in_full, 1)

                    pe.wait_ge(norm_ready, upto(it, u, 2, 2))
                    pe.wait_ge(xn_ready, upto(it, u, 1, 1))
                    pe.wait_ge(weight_done, 2)
                    pixels_and_spectra(0)
                    products(0)
                    pixels_and_spectra(1)
                    transposed(0)
                    products(1)
                    inverse(0)
                    transposed(1)
                    inverse(1)


_OUT = "out_dram"


def kernel(x, L0_conv_conv_w, L0_conv_conv_b, L0_conv_bias, L1_conv_weight_re, L1_conv_weight_im):
    import numpy as _np
    import concourse.bacc as _bacc
    from concourse import mybir as _mybir
    from concourse.bass_utils import run_bass_kernel_spmd as _run

    x = _np.ascontiguousarray(x)
    cw = _np.asarray(L0_conv_conv_w).transpose(1, 2, 0)
    cw0 = _np.zeros((2, C, 2, C), _np.float32)
    cw1 = _np.zeros((2, C, 2, C), _np.float32)
    cw0[0, :, 0], cw0[1, :, 0], cw0[1, :, 1] = cw[:, 0], cw[:, 1], cw[:, 0]
    cw1[0, :, 0], cw1[0, :, 1], cw1[1, :, 1] = cw[:, 2], cw[:, 1], cw[:, 2]
    mix = _np.zeros((2, C, 2, K0, C), _np.float32)
    mix[0, :, 0], mix[1, :, 1] = cw, cw
    wre = _np.asarray(L1_conv_weight_re).transpose(1, 2, 3, 0)
    wim = _np.asarray(L1_conv_weight_im).transpose(1, 2, 3, 0)
    p_w = _np.zeros((2, C, SLOTS, 2, C), _np.float32)
    q_w = _np.zeros((2, C, SLOTS, 2, C), _np.float32)
    for n, (k, l, cplx) in enumerate(frequency_slots()):
        for lane, f in enumerate((k, l)):
            m = ((-f[0]) % N_FREQ, (-f[1]) % N_FREQ)
            p_w[lane, :, n, lane], q_w[lane, :, n, lane] = wre[:, f[0], f[1]], wre[:, m[0], m[1]]
            if cplx:
                a, b = wim[:, f[0], f[1]], wim[:, m[0], m[1]]
                p_w[lane, :, n, 1 - lane], q_w[lane, :, n, 1 - lane] = (a, b) if lane == 0 else (b, a)
    arrays = {
        "x": x, "p_w": p_w.reshape(P, SLOTS, P), "q_w": q_w.reshape(P, SLOTS, P), "cw0": cw0.reshape(P, P),
        "cw1": cw1.reshape(P, P), "w_mix": mix.reshape(P, 2 * K0 * C),
        "conv_b": _np.asarray(L0_conv_conv_b).reshape(1, C), "bias": _np.asarray(L0_conv_bias).reshape(1, 1),
    }
    tables = constants()
    for name in ("ident", "ident16", "gmean", "fwd", "inv", "dft", "taps", "rows", "cols"):
        arrays["c_" + name] = tables[name]
    nc = _bacc.Bacc("TRN2", target_bir_lowering=False, num_devices=1)
    args, given = [], {}
    for name, a in arrays.items():
        a = _np.ascontiguousarray(a)
        given[f"in_{name}_dram"] = a
        args.append(nc.dram_tensor(f"in_{name}_dram", a.shape, _mybir.dt.from_np(a.dtype), kind="ExternalInput").ap())
    args.append(nc.dram_tensor(_OUT, x.shape, _mybir.dt.float32, kind="ExternalOutput").ap())
    nc.disable_value_cache = True
    conv_preact_kernel(nc, *args)
    r = _run(nc, [given], core_ids=[0])
    return r.results[0][_OUT]
```

```python
import math

import numpy as np
import concourse.bass as bass
from concourse import mybir
from contextlib import ExitStack

C, H, W = 64, 128, 128
P = 128
GROUPS = 32
EPS = 1e-5
K0 = 3
TRUNC = 16
M_TILE, N_FREQ = 8, 10
TILES = H // M_TILE
PX = N_FREQ * N_FREQ
SLOTS = PX // 2

HALF = H // 2
ROWPAIRS = H // 2
BLOCKS = ROWPAIRS + 1
GCHUNK = 4
GCHUNKS = -(-BLOCKS // GCHUNK)
CONV_FILLS = ROWPAIRS // 4
PAIRS = TILES * TILES // 2
GRP = 2
T1_FILLS = PAIRS // GRP // 4
FW_FILLS = T1_FILLS // 2
FQ_FILLS = -(-SLOTS // 4)
T2_FILLS = C // 4
IN_FILLS = PAIRS // GRP // 8
INV_N = 96


def transform_matrices(inverse):
    n, sign = N_FREQ, 1.0 if inverse else -1.0
    k = np.arange(n)[:, None]
    i = np.arange(n)[None, :]
    ang = sign * 2.0 * np.pi * k * i / n
    ang = (ang + np.pi) % (2.0 * np.pi) - np.pi
    neg = np.zeros((n, n), dtype=bool)
    hi = ang > np.pi / 2
    ang = np.where(hi, ang - np.pi, ang)
    neg |= hi
    lo = ang < -np.pi / 2
    ang = np.where(lo, ang + np.pi, ang)
    neg |= lo
    size = float(2 ** 20)
    lam = np.round(-np.tan(ang / 2.0) * size) / size
    gam = np.round(np.sin(ang) * size) / size
    s = np.where(neg, -1.0, 1.0)
    out = (s * (1.0 + lam * gam), s * (2.0 * lam + gam * lam * lam), s * gam, s * (1.0 + gam * lam))
    return [m.astype(np.float32).astype(np.float64) for m in out]


def frequency_slots():
    slots, seen = [], set()
    for a in range(N_FREQ):
        for b in range(N_FREQ):
            partner = ((-a) % N_FREQ, (-b) % N_FREQ)
            if (a, b) != partner and partner not in seen:
                seen.add((a, b))
                slots.append(((a, b), (a, b), True))
    h = N_FREQ // 2
    slots.append(((0, 0), (0, h), False))
    slots.append(((h, 0), (h, h), False))
    return slots


def constants():
    f32 = np.float32
    out = {}
    out["ident"] = np.eye(P, dtype=f32)
    out["ident16"] = np.eye(P, dtype=np.float16)
    grp = (np.arange(P) % C) // (C // GROUPS)
    out["gmean"] = (grp[:, None] == grp[None, :]).astype(f32) / (2 * C // GROUPS)
    rr, ri, ir, ii = transform_matrices(False)
    re = np.einsum("bj,ai->ijab", rr, rr) + np.einsum("bj,ai->ijab", ir, ri)
    im = np.einsum("bj,ai->ijab", rr, ir) + np.einsum("bj,ai->ijab", ir, ii)
    fwd = np.zeros((P, 2, SLOTS))
    slots = frequency_slots()
    for n, (k, l, cplx) in enumerate(slots):
        fwd[:PX, 0, n] = re[:, :, k[0], k[1]].reshape(-1)
        fwd[:PX, 1, n] = (im if cplx else re)[:, :, l[0], l[1]].reshape(-1)
    out["fwd"] = fwd.reshape(P, PX).astype(f32)
    rr, ri, ir, ii = transform_matrices(True)
    sc = 1.0 / N_FREQ ** 2
    are = (np.einsum("jb,ia->abij", rr, rr) + np.einsum("jb,ia->abij", ir, ri)) * sc
    aim = (np.einsum("jb,ia->abij", ri, rr) + np.einsum("jb,ia->abij", ii, ri)) * sc
    inv = np.zeros((P, INV_N))
    for n, (k, l, cplx) in enumerate(slots):
        a = are[k[0], k[1], 1:1 + M_TILE, 1:1 + M_TILE].reshape(-1)
        b = (aim if cplx else are)[l[0], l[1], 1:1 + M_TILE, 1:1 + M_TILE].reshape(-1)
        half = 1.0 if cplx else 0.5
        inv[2 * n, :64], inv[2 * n + 1, :64] = half * a, half * b
    out["inv"] = inv.astype(f32)
    th = 2 * np.pi / H
    pos, kk = np.arange(H), np.arange(TRUNC)
    e = np.exp(-1j * th * pos[:, None] * kk[None, :])
    out["dft"] = np.stack([e.real, e.imag], -1).reshape(H, 2 * TRUNC).astype(f32)
    r = np.zeros((2, K0, TRUNC, 4, 2, 4, TRUNC, 2))
    for rih in range(2):
        for a in range(K0):
            for kx in range(TRUNC):
                for riw in range(2):
                    z = (1j ** (rih + riw)) * np.exp(-1j * th * a * kx)
                    for q in range(4):
                        r[rih, a, kx, q, riw, q, kx, 0] = z.real
                        r[rih, a, kx, q, riw, q, kx, 1] = z.imag
    out["taps"] = r.reshape(2 * K0, P, P).transpose(1, 0, 2).reshape(P, 2 * K0 * P).astype(f32)
    g = np.zeros((4, 2, 4, TRUNC, 2, H))
    ph = np.exp(1j * th * kk[:, None] * pos[None, :]) / (H * W)
    for q in range(4):
        g[q, 0, q, :, 0], g[q, 0, q, :, 1] = ph.real, -ph.imag
        g[q, 1, q, :, 0], g[q, 1, q, :, 1] = ph.imag, ph.real
    out["rows"] = g.reshape(8, P, H).transpose(1, 0, 2).reshape(P, 8 * H).astype(f32)
    box = sum(np.exp(-1j * th * b * kk) for b in range(K0))
    d = box[:, None] * np.exp(1j * th * kk[:, None] * pos[None, :])
    base = np.stack([d.real, -d.imag], 1).reshape(2 * TRUNC, W)
    hi = base.astype(np.float16)
    lo = (base - hi.astype(np.float64)).astype(np.float16)
    out["cols"] = np.concatenate([hi, lo, hi, lo], 0)
    return out


def conv_preact_kernel(nc, x, p_w, q_w, cw0, cw1, w_mix, conv_b, bias, c_ident, c_ident16, c_gmean, c_fwd,
                       c_inv, c_dft, c_taps, c_rows, c_cols, out):
    f32, f16 = mybir.dt.float32, mybir.dt.float16
    ALU = mybir.AluOpType
    ACT = mybir.ActivationFunctionType
    B = x.shape[0]
    U = 2
    TRIPS = B // U
    x_v = x.rearrange("(n u) c h w -> n u c h w", u=U)
    out_v = out.rearrange("(n u) c h w -> n u c h w", u=U)

    ctx = ExitStack()
    with ctx:
        def sb(name, shape, dt=f32):
            return ctx.enter_context(nc.sbuf_tensor(name, shape, dt))

        def sem(name):
            return ctx.enter_context(nc.semaphore(name))

        xr = [sb(f"xr{u}", [P, HALF, W]) for u in range(U)]
        xh = [sb(f"xh{r}", [P, 4, W]) for r in range(3)]
        g = [sb(f"g{r}", [P, GCHUNK, W + 2]) for r in range(2)]
        s_x = sb("s_x", [P, BLOCKS * W])
        s = s_x[:, :].rearrange("p (r w) -> p r w", w=W)
        spec = s_x[:, 0:SLOTS * P].rearrange("p (f t) -> p f t", t=P)
        tb = [s_x[:, SLOTS * P + 8 * PX * r:SLOTS * P + 8 * PX * (r + 1)] for r in range(2)]
        u2 = sb("u2", [P, (HALF + 2) * (W + 2)])
        xn = u2[:, :].rearrange("p (r w) -> p r w", w=W + 2)
        qt = u2[:, 0:C * P].rearrange("p (t h o) -> p t h o", h=2, o=C)
        ft = u2[:, 0:C * H // 2].bitcast(f16).rearrange("p (h o) -> p h o", o=C)
        wf = sb("wf", [P, SLOTS, P])
        u3 = sb("u3", [P, PX * C])
        yt = u3[:, :].rearrange("p (o k) -> p o k", k=PX)
        q_in = u3[:, :].rearrange("p (f o) -> p f o", o=P)
        a_t = u3[:, 0:2048].rearrange("p (j n) -> p j n", j=4)
        b_t = u3[:, 2048:4096].rearrange("p (k c) -> p k c", c=C)
        g16 = u3[:, 0:4096].bitcast(f16).rearrange("p (o v k) -> p o v k", v=4, k=2 * TRUNC)
        u_t = u3[:, 4096:4608].rearrange("p (q kx n) -> p q kx n", q=4, n=8)
        y_t = u3[:, 4608:6144].rearrange("p (q n) -> p q n", q=4)
        z_t = u3[:, 6144:6400]
        px = [sb(f"px{r}", [P, 4 * P]) for r in range(2)]
        ident, ident16 = sb("ident", [P, P]), sb("ident16", [P, P], f16)
        gmean, fwd, inv = sb("gmean", [P, P]), sb("fwd", [P, PX]), sb("inv", [P, INV_N])
        dft, taps, rows = sb("dft", [P, 2 * TRUNC]), sb("taps", [P, 2 * K0, P]), sb("rows", [P, 8, H])
        cols = sb("cols", [P, W], f16)
        w0, w1, wm = sb("w0", [P, P]), sb("w1", [P, P]), sb("wm", [P, 2 * K0 * C])
        brow, b1 = sb("brow", [1, C]), sb("b1", [1, 1])
        st = sb("st", [P, HALF // 4, 6])
        sm = [sb(f"sm{n}", [P, 12]) for n in range(2)]
        dcs = sb("dcs", [P, 1])
        carry = sb("carry", [P, 3])

        ps = [ctx.enter_context(nc.psum_tensor(f"ps{b}", [P, 512], f32)) for b in range(4)]
        pw = [ctx.enter_context(nc.psum_tensor(f"pw{b}", [P, 2, 512], f32)) for b in range(2)]
        wide = [pw[b // 2][:, b % 2, :] for b in range(4)]

        const_in, weight_in, weight_done = sem("const_in"), sem("weight_in"), sem("weight_done")
        pads_set = sem("pads_set")
        x_in = [sem(f"x_in{u}") for u in range(U)]
        xh_in = [sem(f"xh_in{r}") for r in range(3)]
        x_out = [sem(f"x_out{u}") for u in range(U)]
        xh_read = sem("xh_read")
        vec_step = sem("vec_step")
        stat_ready = sem("stat_ready")
        stat_mean = sem("stat_mean")
        v_ready, sd_ready = sem("v_ready"), sem("sd_ready")
        norm_ready = sem("norm_ready")
        pool_step = sem("pool_step")
        g_used = sem("g_used")
        a_done = sem("a_done")
        b_full, b_done = sem("b_full"), sem("b_done")
        uu_full, uu_done = sem("uu_full"), sem("uu_done")
        y_full, y_done = sem("y_full"), sem("y_done")
        z_full, z_done = sem("z_full"), sem("z_done")
        gg_full, hi_done, lo_done = sem("gg_full"), sem("hi_done"), sem("lo_done")
        dup_done = sem("dup_done")
        ft_full, ft_done = sem("ft_full"), sem("ft_done")
        conv_full, conv_done = sem("conv_full"), sem("conv_done")
        xn_ready = sem("xn_ready")
        tb_ready = sem("tb_ready")
        t1_full, t1_done = sem("t1_full"), sem("t1_done")
        px_used = sem("px_used")
        fw_even, fw_odd = sem("fw_even"), sem("fw_odd")
        fq_full, fq_done = sem("fq_full"), sem("fq_done")
        t2_full, t2_done = sem("t2_full"), sem("t2_done")
        in_full, in_done = sem("in_full"), sem("in_done")

        T1_ALL, FW_ALL, FQ_ALL = GRP * T1_FILLS, GRP * FW_FILLS, GRP * FQ_FILLS
        TB_ALL = T1_ALL // 2
        T2_ALL, IN_ALL = GRP * T2_FILLS, GRP * IN_FILLS
        XH_CHUNKS = C // 4
        BANDS = 4
        LAST = TRIPS - 1

        def upto(it, u, per_image, k=0):
            return it * (U * per_image) + (u * per_image + k)

        def windows(row, col):
            return bass.AP(tensor=u2[:, :].tensor, offset=row * (W + 2) + col,
                           ap=[[(HALF + 2) * (W + 2), P], [M_TILE, 8], [W + 2, N_FREQ], [1, N_FREQ]])

        def apart(eng, h=0):
            if eng is nc.gpsimd:
                col = carry[C * h:C * h + 16, :]
                eng.tensor_tensor(col[:, 0:1], col[:, 2:3], col[:, 2:3], ALU.add)
            else:
                eng.tensor_copy(carry[:, 1:2], carry[:, 2:3])

        def trips(eng, image):
            if LAST > 0:
                with eng.Fori(0, LAST) as it:
                    for u in range(U):
                        image(it, u, True)
            image(LAST, 0, True)
            image(LAST, 1, False)

        block = ctx.enter_context(nc.Block())

        @block.sync
        def _(sp):
            def image(it, u, first):
                if not first:
                    sp.wait_ge(x_out[u], it * 64)
                for h in range(2):
                    sp.dma_start(xr[u][C * h:C * h + C, :, :],
                                 x_v[it, u, :, HALF * h:HALF * h + HALF, :]).then_inc(x_in[u], 16)
                for n in range(XH_CHUNKS):
                    m = u * XH_CHUNKS + n
                    if m >= 3:
                        sp.wait_ge(xh_read, upto(it, u, XH_CHUNKS, n - 2))
                    elif not first:
                        sp.wait_ge(xh_read, it * (U * XH_CHUNKS))
                    sp.dma_start(xh[m % 3][:, :, :],
                                 x_v[it, u, 4 * n:4 * n + 4, :, :].rearrange("c h w -> h c w")
                                 ).then_inc(xh_in[m % 3], 16)

            sp.dma_start(gmean[:, :], c_gmean).then_inc(const_in, 16)
            for dst, src in ((ident, c_ident), (dft, c_dft), (ident16, c_ident16),
                             (cols, c_cols), (w0, cw0), (w1, cw1), (wm, w_mix), (fwd, c_fwd), (inv, c_inv),
                             (brow, conv_b), (b1, bias)):
                sp.dma_start(dst[:, :], src).then_inc(const_in, 16)
            sp.dma_start(taps[:, :, :], c_taps.rearrange("p (a m) -> p a m", m=P)).then_inc(const_in, 16)
            sp.dma_start(rows[:, :, :], c_rows.rearrange("p (a m) -> p a m", m=H)).then_inc(const_in, 16)
            sp.dma_start(wf[:, :, :], p_w).then_inc(weight_in, 16)
            sp.dma_start(q_in, q_w).then_inc(weight_in, 16)
            for u in range(U):
                image(0, u, True)
            if LAST > 0:
                with sp.Fori(1, TRIPS) as it:
                    for u in range(U):
                        image(it, u, False)

        def staggered(n):
            pieces = []
            for par in range(2):
                j, nb = 0, min(GCHUNK, BLOCKS - GCHUNK * n)
                while j < nb:
                    row = 2 * (GCHUNK * n + j) - 1 + par
                    cnt = 1
                    if 0 <= row < H:
                        while j + cnt < nb and row + 2 * cnt < H and (row + 2 * cnt) // HALF == row // HALF:
                            cnt += 1
                        pieces.append((par, j, cnt, row // HALF, row % HALF))
                    else:
                        pieces.append((par, j, cnt, None, None))
                    j += cnt
            return pieces

        POOL = sum(len(staggered(n)) for n in range(GCHUNKS))

        @block.gpsimd
        def _(pool):
            def normalise(it, u):
                x1, steps = xr[u % U], 0
                pool.wait_ge(norm_ready, upto(it, u, 2, 1))
                for n in range(GCHUNKS):
                    k = u * GCHUNKS + n
                    if k >= 2:
                        pool.wait_ge(g_used, upto(it, u, GCHUNKS, n - 1))
                    for par, j, cnt, h, lr in staggered(n):
                        if k or steps:
                            pool.wait_ge(pool_step, upto(it, u, POOL, steps))
                        apart(pool, par if h is None else h)
                        dst = g[k % 2][C * par:C * par + C, j:j + cnt, 1:W + 1]
                        if h is None:
                            pool.memset(dst, 0.0).then_inc(pool_step, 1)
                        else:
                            pool.tensor_scalar(dst, x1[C * h:C * h + C, lr:lr + 2 * cnt - 1:2, :],
                                               sm[0][C * h:C * h + C, 6:7], sm[0][C * h:C * h + C, 8:9],
                                               ALU.mult, ALU.add).then_inc(pool_step, 1)
                        steps += 1

            def store(it, u, grp):
                pool.wait_ge(in_done, upto(it, u, IN_ALL, (grp + 1) * IN_FILLS))
                for h in range(2):
                    lr = grp * HALF // 2
                    pool.dma_start(out_v[it, u, :, HALF * h + lr:HALF * h + lr + HALF // 2, :],
                                   xr[u][C * h:C * h + C, lr:lr + HALF // 2, :]).then_inc(x_out[u], 16)

            def image(it, u, more):
                if more:
                    normalise(it, u + 1)
                store(it, u, 0)
                store(it, u, 1)

            pool.wait_ge(pads_set, 1)
            normalise(0, 0)
            trips(pool, image)
            for u in range(U):
                pool.wait_ge(x_out[u], 64 * TRIPS)

        VEC = 2 * (1 + 1 + 4) + 1 + GCHUNKS + 1

        @block.vector
        def _(dve):
            chain = [0]
            where = [0, 0]

            def link(ins):
                chain[0] += 1
                ins.then_inc(vec_step, 1)
                dve.wait_ge(vec_step, where[0] * (U * VEC) + where[1] + chain[0])

            def rowstats(x1, m):
                return dve.bn_stats(st[:, m, :], x1[:, 4 * m:4 * m + 4, :].rearrange("p r w -> p (r w)"))

            def average(n, last):
                link(last)
                apart(dve)
                dve.bn_aggr(sm[n][:, 0:2], st[:, :, :]).then_inc(stat_ready, 1)

            def spread(it, u, n):
                m = sm[n]
                dve.wait_ge(stat_mean, upto(it, u, 4, 2 * n + 1))
                dve.tensor_copy(m[:, 9:10], ps[1][:, 0:1])
                link(dve.tensor_tensor(m[:, 2:3], m[:, 0:1], ps[1][:, 0:1], ALU.subtract))
                dve.scalar_tensor_tensor(m[:, 3:4], m[:, 2:3], m[:, 2:3], m[:, 1:2],
                                         ALU.mult, ALU.add).then_inc(stat_ready, 1)

            def variance(it, u, n):
                dve.wait_ge(stat_mean, upto(it, u, 4, 2 * n + 2))
                dve.tensor_scalar(sm[n][:, 4:5], ps[0][:, 0:1], EPS, None, ALU.add).then_inc(v_ready, 1)

            def scale(it, u, n):
                m = sm[n]
                dve.wait_ge(sd_ready, upto(it, u, 2, n + 1))
                link(dve.reciprocal(m[:, 6:7], m[:, 5:6]))
                link(dve.tensor_scalar(m[:, 7:8], m[:, 6:7], m[:, 6:7], m[:, 4:5], ALU.mult, ALU.mult))
                link(dve.tensor_scalar(m[:, 7:8], m[:, 7:8], -0.5, 1.5, ALU.mult, ALU.add))
                link(dve.tensor_scalar(m[:, 6:7], m[:, 6:7], m[:, 7:8], None, ALU.mult))
                return dve.tensor_scalar(m[:, 8:9], m[:, 9:10], m[:, 6:7], -1.0, ALU.mult, ALU.mult)

            def statistics(it, u):
                dve.wait_ge(x_in[u % U], it * 32 + 32 * (1 + u // U))
                for m in range(HALF // 4):
                    last = rowstats(xr[u % U], m)
                average(0, last)

            def constant_term(it, u):
                link(scale(it, u, 0))
                dve.tensor_scalar(dcs[0:C, :], sm[0][0:C, 8:9], float(H * W), None, ALU.mult).then_inc(norm_ready, 1)

            def box(it, u, n):
                nb = min(GCHUNK, BLOCKS - GCHUNK * n)
                dve.wait_ge(pool_step, upto(it, u, POOL, sum(len(staggered(m)) for m in range(n + 1))))
                src, dst = g[(u * GCHUNKS + n) % 2], s[:, GCHUNK * n:GCHUNK * n + nb, :]
                link(dve.tensor_tensor(dst, src[:, 0:nb, 0:W], src[:, 0:nb, 1:W + 1], ALU.add))
                dve.tensor_tensor(dst, dst, src[:, 0:nb, 2:W + 2], ALU.add).then_inc(g_used, 1)

            def mixed(it, u):
                for q in range(4):
                    dve.wait_ge(y_full, upto(it, u, 4, q + 1))
                    dve.tensor_copy(y_t[:, q, :], wide[q][:, 0:2 * K0 * C]).then_inc(y_done, 1)

            def summed(it, u):
                dve.wait_ge(z_full, upto(it, u, 1, 1))
                link(dve.tensor_copy(z_t, wide[0][:, 0:4 * C]))
                dve.tensor_tensor(z_t[0:1, 0:C], z_t[0:1, 0:C], brow[:, :], ALU.add).then_inc(z_done, 1)

            def low_parts(it, u):
                for q in range(4):
                    dve.wait_ge(hi_done, upto(it, u, 4, q + 1))
                    dst = g16.rearrange("p o v (kg q r) -> p v q r kg o", q=4, r=2)
                    src = wide[q].rearrange("p (r kg o) -> p r kg o", r=2, kg=4)
                    dve.tensor_tensor(dst[:, 2, q, :], src, dst[:, 0, q, :], ALU.subtract).then_inc(lo_done, 1)

            def coefficients(it, u):
                for n in range(8):
                    dve.wait_ge(ft_full, upto(it, u, 8, n + 1))
                    dve.tensor_copy(ft[:, :, 8 * n:8 * n + 8].rearrange("p h o -> p o h"),
                                    ps[2 + n % 2][:, :].bitcast(f16).rearrange("p (o h) -> p o h", h=H)
                                    ).then_inc(ft_done, 1)

            def convolved(it, u):
                for n in range(CONV_FILLS):
                    h, j = n % 2, n // 2
                    dve.wait_ge(conv_full, upto(it, u, CONV_FILLS, n + 1))
                    for par in range(2):
                        dst = xr[u][C * h:C * h + C, 8 * j + par:8 * j + 8:2, :]
                        ins = dve.tensor_tensor(dst, ps[n % 2][C * par:C * par + C, :].rearrange("p (r w) -> p r w", w=W),
                                                dst, ALU.add)
                    ins.then_inc(conv_done, 1)
                    if h == 0 and j:
                        dve.wait_ge(conv_done, upto(it, u, CONV_FILLS, n))
                        rowstats(xr[u], 2 * j - 2)
                        rowstats(xr[u], 2 * j - 1)
                dve.wait_ge(conv_done, upto(it, u, CONV_FILLS, CONV_FILLS))
                rowstats(xr[u], 14)
                average(1, rowstats(xr[u], 15))
                dve.memset(xn[:, :, 0:1], 0.0)
                dve.memset(xn[:, :, W + 1:W + 2], 0.0)
                dve.memset(xn[0:C, 0:1, 1:W + 1], 0.0)
                dve.memset(xn[C:P, HALF + 1:HALF + 2, 1:W + 1], 0.0)
                spread(it, u, 1)
                variance(it, u, 1)
                scale(it, u, 1).then_inc(norm_ready, 1)

            def gather(it, u, n):
                th, tw = 8 * n // TILES, 8 * n % TILES
                if n >= 2:
                    dve.wait_ge(t1_full, upto(it, u, T1_ALL, 2 * (n - 1)))
                dve.wait_ge(xn_ready, upto(it, u, 1 + BANDS, 1 + min(BANDS, (8 * th + 8) // (HALF // BANDS) + 1)))
                dve.tensor_copy(tb[n % 2].rearrange("p (t y x) -> p t y x", t=8, y=N_FREQ),
                                windows(M_TILE * th, M_TILE * tw)).then_inc(tb_ready, 1)

            def spectra(it, u, grp):
                for n in range(FW_FILLS):
                    k = grp * FW_FILLS + n
                    if k + 2 < TB_ALL:
                        gather(it, u, k + 2)
                    if n % 2:
                        continue
                    dve.wait_ge(px_used, upto(it, u, T1_ALL, 2 * (k + 1)))
                    if n == 0 and grp > 0:
                        dve.wait_ge(fq_full, upto(it, u, FQ_ALL, grp * FQ_FILLS))
                    for h in range(2):
                        src = pw[0][C * h:C * h + C, :, 0:4 * PX].rearrange("p b (t v f) -> p v f b t", v=2, f=SLOTS)
                        for v in range(2):
                            dst = spec[C * v:C * v + C, :, 64 * h + 8 * n:64 * h + 8 * n + 8].rearrange("p f (b t) -> p f b t", b=2)
                            ins = dve.tensor_copy(dst, src[:, v])
                    ins.then_inc(fw_even, 1)

            def result(it, u, grp, n):
                dve.wait_ge(in_full, upto(it, u, IN_ALL, grp * IN_FILLS + n + 1))
                th, tw = (grp * 64 + 8 * n) // TILES, (8 * n) % TILES
                dst = xr[u][:, M_TILE * th:M_TILE * th + M_TILE, M_TILE * tw:M_TILE * tw + 64].rearrange(
                    "p y (t x) -> p t y x", t=8)
                src = ps[n % 2][:, :].rearrange("p (t y x) -> p t y x", t=8, y=M_TILE)
                dve.tensor_tensor(dst, src, dst, ALU.add).then_inc(in_done, 1)

            def image(it, u, more):
                where[0], where[1], chain[0] = it, (u + 1) * VEC, 0
                coefficients(it, u)
                convolved(it, u)
                gather(it, u, 0)
                gather(it, u, 1)
                spectra(it, u, 0)
                if more:
                    statistics(it, u + 1)
                    spread(it, u + 1, 0)
                spectra(it, u, 1)
                if more:
                    variance(it, u + 1, 0)
                    constant_term(it, u + 1)
                    dve.wait_ge(fq_full, upto(it, u, FQ_ALL, FQ_ALL))
                for n in range(IN_FILLS):
                    result(it, u, 0, n)
                    if more:
                        box(it, u + 1, 2 * n)
                        box(it, u + 1, 2 * n + 1)
                if more:
                    box(it, u + 1, GCHUNKS - 1)
                for n in range(IN_FILLS):
                    if more and n == 3:
                        mixed(it, u + 1)
                    if more and n == 4:
                        summed(it, u + 1)
                    if more and n == 6:
                        low_parts(it, u + 1)
                    result(it, u, 1, n)
                assert not more or chain[0] == VEC, chain[0]

            dve.memset(u2[:, :], 0.0)
            for r in range(2):
                dve.memset(g[r][:, :, 0:1], 0.0)
                dve.memset(g[r][:, :, W + 1:W + 2], 0.0)
                dve.memset(px[r][96:P, :], 0.0)
            dve.memset(carry[:, :], 0.0)
            dve.memset(dcs[:, :], 0.0).then_inc(pads_set, 1)
            dve.wait_ge(pads_set, 1)
            dve.wait_ge(weight_in, 32)
            for lo_p, lo_c, op in ((0, 0, ALU.add), (C, C, ALU.add), (0, C, ALU.subtract), (C, 0, ALU.subtract)):
                blk = wf[lo_p:lo_p + C, :, lo_c:lo_c + C]
                ins = dve.tensor_tensor(blk, blk, q_in[lo_p:lo_p + C, :, lo_c:lo_c + C], op)
            ins.then_inc(weight_done, 1)
            dve.wait_ge(const_in, 16 * 14)
            dve.tensor_scalar(brow[:, :], brow[:, :], b1[:, :], float(H * W) / K0, ALU.add, ALU.mult).then_inc(weight_done, 1)
            dve.wait_ge(weight_done, 2)
            statistics(0, 0)
            spread(0, 0, 0)
            variance(0, 0, 0)
            constant_term(0, 0)
            for n in range(GCHUNKS):
                box(0, 0, n)
            mixed(0, 0)
            summed(0, 0)
            low_parts(0, 0)
            dve.engine_nop().then_inc(vec_step, VEC - chain[0])
            trips(dve, image)

        @block.scalar
        def _(act):
            def root(it, u, n):
                act.wait_ge(v_ready, upto(it, u, 2, n + 1))
                act.activation(sm[n][:, 5:6], sm[n][:, 4:5], ACT.Sqrt).then_inc(sd_ready, 1)

            def rows_dft(it, u):
                for q in range(4):
                    act.wait_ge(xh_read, upto(it, u, XH_CHUNKS, 4 * (q + 1)))
                    act.copy(a_t[:, q, :], wide[q]).then_inc(a_done, 1)

            def rows_dft_transposed(it, u):
                for q in range(4):
                    act.wait_ge(b_full, upto(it, u, 4, q + 1))
                    dst = b_t[:, :, 16 * q:16 * q + 16].rearrange("p k (g cc) -> p cc g k", cc=4)
                    src = ps[2 + q % 2][:, :].rearrange("p (cc g k) -> p cc g k", cc=4, g=4)
                    act.copy(dst, src).then_inc(b_done, 1)

            def spectrum(it, u):
                act.wait_ge(norm_ready, upto(it, u, 2, 1))
                act.wait_ge(uu_full, upto(it, u, 1, 1))
                act.activation(u_t, wide[0].rearrange("p (kx q n) -> p q kx n", q=4, n=8), ACT.Copy,
                               scale=sm[0][:, 6:7]).then_inc(uu_done, 1)
                act.wait_ge(uu_done, upto(it, u, 2, 1))
                act.activation(u_t[:, 0, 0, 0:1], u_t[:, 0, 0, 0:1], ACT.Identity, bias=dcs[:, :]).then_inc(uu_done, 1)

            def high_parts(it, u):
                dst = g16.rearrange("p o v (kg q r) -> p v q r kg o", q=4, r=2)
                for q in range(4):
                    act.wait_ge(gg_full, upto(it, u, 4, q + 1))
                    src = wide[q].rearrange("p (r kg o) -> p r kg o", r=2, kg=4)
                    act.copy(dst[:, 0, q, :], src)
                    act.copy(dst[:, 1, q, :], src).then_inc(hi_done, 1)
                act.wait_ge(lo_done, upto(it, u, 4, 4))
                act.copy(g16[:, :, 3, :], g16[:, :, 2, :]).then_inc(dup_done, 1)

            def normalised(it, u):
                act.wait_ge(norm_ready, upto(it, u, 2, 2))
                sc, sh = sm[1][:, 6:7], sm[1][:, 8:9]
                act.activation(xn[C:P, 0, 1:W + 1], xr[u][0:C, HALF - 1, :], ACT.Identity, bias=sh[0:C], scale=sc[0:C])
                act.activation(xn[0:C, HALF + 1, 1:W + 1], xr[u][C:P, 0, :], ACT.Identity, bias=sh[C:P],
                               scale=sc[C:P]).then_inc(xn_ready, 1)
                n = HALF // BANDS
                for b in range(BANDS):
                    act.activation(xn[:, n * b + 1:n * b + n + 1, 1:W + 1], xr[u][:, n * b:n * b + n, :],
                                   ACT.Identity, bias=sh, scale=sc).then_inc(xn_ready, 1)

            def pixels_and_spectra(it, u, grp):
                for n in range(T1_FILLS + 1):
                    if n < T1_FILLS:
                        k = grp * T1_FILLS + n
                        act.wait_ge(t1_full, upto(it, u, T1_ALL, k + 1))
                        if k >= 2:
                            act.wait_ge(px_used, upto(it, u, T1_ALL, k - 1))
                        act.copy(px[n % 2][0:PX, :], ps[2 + n % 2][0:PX, :]).then_inc(t1_done, 1)
                    if n >= 4 and n % 4 == 0:
                        m = n // 2 - 1
                        k = grp * FW_FILLS + m
                        act.wait_ge(px_used, upto(it, u, T1_ALL, 2 * (k + 1)))
                        if m == 1 and grp > 0:
                            act.wait_ge(fq_full, upto(it, u, FQ_ALL, grp * FQ_FILLS))
                        for h in range(2):
                            src = pw[1][C * h:C * h + C, :, 0:4 * PX].rearrange("p b (t v f) -> p v f b t", v=2, f=SLOTS)
                            for v in range(2):
                                dst = spec[C * v:C * v + C, :, 64 * h + 8 * m:64 * h + 8 * m + 8].rearrange("p f (b t) -> p f b t", b=2)
                                ins = act.copy(dst, src[:, v])
                        ins.then_inc(fw_odd, 1)

            def products(it, u, grp):
                for n in range(FQ_FILLS):
                    k = grp * FQ_FILLS + n
                    nf = min(4, SLOTS - 4 * n)
                    act.wait_ge(fq_full, upto(it, u, FQ_ALL, k + 1))
                    if n == 0:
                        if grp:
                            act.wait_ge(t2_full, upto(it, u, T2_ALL, grp * T2_FILLS))
                        else:
                            act.wait_ge(ft_full, upto(it, u, 8, 8))
                    src = wide[n % 4][:, 0:nf * P].rearrange("p (f v o) -> p f v o", f=nf, v=2)
                    dst = yt[:, :, 8 * n:8 * n + 2 * nf].rearrange("p o (f v) -> p f v o", v=2)
                    act.copy(dst, src).then_inc(fq_done, 1)

            def transposed(it, u, grp):
                for n in range(T2_FILLS):
                    k = grp * T2_FILLS + n
                    act.wait_ge(t2_full, upto(it, u, T2_ALL, k + 1))
                    if n == 0 and grp == 0:
                        act.wait_ge(tb_ready, upto(it, u, TB_ALL, TB_ALL))
                    elif n == 0:
                        act.wait_ge(in_full, upto(it, u, IN_ALL, IN_FILLS))
                    act.copy(qt[0:PX, :, :, 4 * n:4 * n + 4].rearrange("p t h o -> p o h t"),
                             ps[2 + n % 2][0:PX, :].rearrange("p (o h t) -> p o h t", o=4, h=2)).then_inc(t2_done, 1)

            def image(it, u, more):
                root(it, u, 1)
                normalised(it, u)
                pixels_and_spectra(it, u, 0)
                products(it, u, 0)
                pixels_and_spectra(it, u, 1)
                if more:
                    root(it, u + 1, 0)
                transposed(it, u, 0)
                products(it, u, 1)
                transposed(it, u, 1)
                if more:
                    rows_dft(it, u + 1)
                    rows_dft_transposed(it, u + 1)
                    spectrum(it, u + 1)
                    high_parts(it, u + 1)

            act.wait_ge(pads_set, 1)
            act.wait_ge(weight_done, 2)
            root(0, 0, 0)
            rows_dft(0, 0)
            rows_dft_transposed(0, 0)
            spectrum(0, 0)
            high_parts(0, 0)
            trips(act, image)

        @block.tensor
        def _(pe):
            def mean(it, u, n, j):
                pe.wait_ge(stat_ready, upto(it, u, 4, 2 * n + j + 1))
                pe.matmul(ps[1 - j][:, 0:1], gmean[:, :], sm[n][:, 0:1] if j == 0 else sm[n][:, 3:4],
                          start=True, stop=True).then_inc(stat_mean, 1)

            def rows_dft(it, u, n):
                q, gq = n // 4, n % 4
                m = (u % U) * XH_CHUNKS + n
                per_trip = len(range(m % 3, U * XH_CHUNKS, 3))
                pe.wait_ge(xh_in[m % 3], it * (16 * per_trip) + 16 * (m // 3 + 1 + (u // U) * per_trip))
                pe.matmul(wide[q][32 * gq:32 * gq + 32, :], dft[:, :], xh[m % 3][:, :, :].rearrange("p c w -> p (c w)"),
                          start=True, stop=True).then_inc(xh_read, 1)

            def rows_dft_transposed(it, u):
                for q in range(4):
                    pe.wait_ge(a_done, upto(it, u, 4, q + 1))
                    if q >= 2:
                        pe.wait_ge(b_done, upto(it, u, 4, q - 1))
                    for cc in range(4):
                        ins = pe.transpose(ps[2 + q % 2][:, P * cc:P * cc + P], a_t[:, q, P * cc:P * cc + P], ident[:, :])
                    ins.then_inc(b_full, 1)

            def columns_dft(it, u):
                pe.wait_ge(b_done, upto(it, u, 4, 4))
                for kx in range(TRUNC):
                    ins = pe.matmul(wide[0][:, 32 * kx:32 * kx + 32], b_t[:, 2 * kx:2 * kx + 2, :].rearrange("p k c -> p (k c)"),
                                    dft[:, :], start=True, stop=True)
                ins.then_inc(uu_full, 1)

            def mix(it, u):
                pe.wait_ge(uu_done, upto(it, u, 2, 2))
                for q in range(4):
                    pe.matmul(wide[q][:, 0:2 * K0 * C], u_t[:, q, :, :].rearrange("p kx n -> p (kx n)"), wm[:, :],
                              start=True, stop=True).then_inc(y_full, 1)

            def sum_taps(it, u):
                pe.wait_ge(y_done, upto(it, u, 4, 4))
                for n in range(2 * K0):
                    ins = pe.matmul(wide[0][:, 0:4 * C].rearrange("p (q o) -> p q o", o=C), taps[:, n, :],
                                    y_t[:, :, C * n:C * n + C], start=(n == 0), stop=(n == 2 * K0 - 1))
                ins.then_inc(z_full, 1)

            def rows_inverse(it, u):
                pe.wait_ge(z_done, upto(it, u, 1, 1))
                for q in range(4):
                    for r in range(2):
                        ins = pe.matmul(wide[q][:, 4 * C * r:4 * C * r + 4 * C], rows[:, 2 * q + r, :], z_t,
                                        start=True, stop=True)
                    ins.then_inc(gg_full, 1)

            def coefficients(it, u):
                pe.wait_ge(dup_done, upto(it, u, 1, 1))
                for n in range(8):
                    if n >= 2:
                        pe.wait_ge(ft_done, upto(it, u, 8, n - 1))
                    bank = ps[2 + n % 2][:, :].bitcast(f16)
                    for j in range(8):
                        ins = pe.transpose(bank[:, P * j:P * j + P], g16[:, 8 * n + j, :, :].rearrange("p v k -> p (v k)"),
                                           ident16[:, :])
                    ins.then_inc(ft_full, 1)

            def convolve(it, u):
                pe.wait_ge(g_used, upto(it, u, GCHUNKS, GCHUNKS))
                for n in range(CONV_FILLS):
                    h, j = n % 2, n // 2
                    r = 32 * h + 4 * j
                    if n >= 2:
                        pe.wait_ge(conv_done, upto(it, u, CONV_FILLS, n - 1))
                    bank = ps[n % 2]
                    pe.matmul(bank[:, :], w0[:, :], s[:, r:r + 4, :].rearrange("p r w -> p (r w)"), start=True, stop=False)
                    pe.matmul(bank[:, :], w1[:, :], s[:, r + 1:r + 5, :].rearrange("p r w -> p (r w)"), start=False, stop=False)
                    if n == 0:
                        pe.wait_ge(ft_done, upto(it, u, 8, 8))
                    for i in range(4):
                        ins = pe.matmul(bank[:, W * i:W * i + W],
                                        ft[:, 2 * (r + i):2 * (r + i) + 2, :].rearrange("p par o -> p (par o)"),
                                        cols[:, :], start=False, stop=(i == 3))
                    ins.then_inc(conv_full, 1)
                pe.wait_ge(conv_done, upto(it, u, CONV_FILLS, CONV_FILLS))

            def pixels_and_spectra(it, u, grp):
                for n in range(T1_FILLS + 1):
                    if n < T1_FILLS:
                        k = grp * T1_FILLS + n
                        if k >= 2:
                            pe.wait_ge(t1_done, upto(it, u, T1_ALL, k - 1))
                        pe.wait_ge(tb_ready, upto(it, u, TB_ALL, k // 2 + 1))
                        for j in range(4):
                            tile = tb[(k // 2) % 2][:, PX * (4 * (k % 2) + j):PX * (4 * (k % 2) + j) + PX]
                            ins = pe.transpose(ps[2 + n % 2][0:PX, P * j:P * j + P], tile, ident[:, :])
                        ins.then_inc(t1_full, 1)
                    if n >= 1:
                        m = n - 1
                        k = grp * FW_FILLS + m // 2
                        if m % 2 == 0 and k >= 2:
                            pe.wait_ge(fw_odd if k % 2 else fw_even, upto(it, u, FW_ALL // 2, k // 2))
                        if m == 0 and grp == 1:
                            pe.wait_ge(fq_done, upto(it, u, FQ_ALL, FQ_FILLS))
                        pe.wait_ge(t1_done, upto(it, u, T1_ALL, grp * T1_FILLS + m + 1))
                        for j in range(4):
                            ins = pe.matmul(pw[(m // 2) % 2][:, m % 2, PX * j:PX * j + PX],
                                            px[m % 2][:, P * j:P * j + P], fwd[:, :], start=True, stop=True)
                        ins.then_inc(px_used, 1)

            def products(it, u, grp):
                pe.wait_ge(fw_even, upto(it, u, FW_ALL // 2, (grp + 1) * FW_FILLS // 2))
                pe.wait_ge(fw_odd, upto(it, u, FW_ALL // 2, (grp + 1) * FW_FILLS // 2))
                for n in range(FQ_FILLS):
                    k = grp * FQ_FILLS + n
                    if n >= 4:
                        pe.wait_ge(fq_done, upto(it, u, FQ_ALL, k - 3))
                    for j in range(min(4, SLOTS - 4 * n)):
                        ins = pe.matmul(wide[n % 4][:, P * j:P * j + P], spec[:, 4 * n + j, :], wf[:, 4 * n + j, :],
                                        start=True, stop=True)
                    ins.then_inc(fq_full, 1)

            def transpose(it, u, grp):
                pe.wait_ge(fq_done, upto(it, u, FQ_ALL, (grp + 1) * FQ_FILLS))
                for n in range(T2_FILLS):
                    k = grp * T2_FILLS + n
                    if k >= 2:
                        pe.wait_ge(t2_done, upto(it, u, T2_ALL, k - 1))
                    for j in range(4):
                        ins = pe.transpose(ps[2 + n % 2][0:PX, P * j:P * j + P], yt[:, 4 * n + j, :], ident[:, :])
                    ins.then_inc(t2_full, 1)

            def inverse(it, u, grp, n):
                k = grp * IN_FILLS + n
                if k >= 2:
                    pe.wait_ge(in_done, upto(it, u, IN_ALL, k - 1))
                for j in range(8):
                    t = 8 * n + j
                    nn = INV_N if j < 7 else 64
                    ins = pe.matmul(ps[n % 2][:, 64 * j:64 * j + nn], qt[:, t, :, :].rearrange("p h o -> p (h o)"),
                                    inv[:, 0:nn], start=True, stop=True)
                ins.then_inc(in_full, 1)

            def image(it, u, more):
                coefficients(it, u)
                convolve(it, u)
                mean(it, u, 1, 0)
                mean(it, u, 1, 1)
                pixels_and_spectra(it, u, 0)
                products(it, u, 0)
                if more:
                    mean(it, u + 1, 0, 0)
                pixels_and_spectra(it, u, 1)
                if more:
                    mean(it, u + 1, 0, 1)
                transpose(it, u, 0)
                products(it, u, 1)
                pe.wait_ge(t2_done, upto(it, u, T2_ALL, T2_FILLS))
                if more:
                    pe.wait_ge(v_ready, upto(it, u + 1, 2, 1))
                    pe.wait_ge(fq_done, upto(it, u, FQ_ALL, FQ_ALL))
                for n in range(IN_FILLS):
                    inverse(it, u, 0, n)
                    if more:
                        rows_dft(it, u + 1, 2 * n)
                        rows_dft(it, u + 1, 2 * n + 1)
                transpose(it, u, 1)
                pe.wait_ge(t2_done, upto(it, u, T2_ALL, T2_ALL))
                for n in range(IN_FILLS):
                    inverse(it, u, 1, n)
                    if more and n == 0:
                        rows_dft_transposed(it, u + 1)
                    if more and n == 1:
                        columns_dft(it, u + 1)
                    if more and n == 2:
                        mix(it, u + 1)
                    if more and n == 3:
                        sum_taps(it, u + 1)
                    if more and n == 5:
                        rows_inverse(it, u + 1)
                pe.wait_ge(in_done, upto(it, u, IN_ALL, IN_ALL))

            pe.wait_ge(const_in, 16 * 14)
            mean(0, 0, 0, 0)
            mean(0, 0, 0, 1)
            for n in range(XH_CHUNKS):
                rows_dft(0, 0, n)
            pe.wait_ge(weight_done, 2)
            rows_dft_transposed(0, 0)
            columns_dft(0, 0)
            mix(0, 0)
            sum_taps(0, 0)
            rows_inverse(0, 0)
            trips(pe, image)


_OUT = "out_dram"


def kernel(x, L0_conv_conv_w, L0_conv_conv_b, L0_conv_bias, L1_conv_weight_re, L1_conv_weight_im):
    import numpy as _np
    import concourse.bacc as _bacc
    from concourse import mybir as _mybir
    from concourse.bass_utils import run_bass_kernel_spmd as _run

    x = _np.ascontiguousarray(x)
    cw = _np.asarray(L0_conv_conv_w).transpose(1, 2, 0)
    cw0 = _np.zeros((2, C, 2, C), _np.float32)
    cw1 = _np.zeros((2, C, 2, C), _np.float32)
    cw0[0, :, 0], cw0[1, :, 0], cw0[1, :, 1] = cw[:, 0], cw[:, 1], cw[:, 0]
    cw1[0, :, 0], cw1[0, :, 1], cw1[1, :, 1] = cw[:, 2], cw[:, 1], cw[:, 2]
    mix = _np.zeros((2, C, 2, K0, C), _np.float32)
    mix[0, :, 0], mix[1, :, 1] = cw, cw
    wre = _np.asarray(L1_conv_weight_re).transpose(1, 2, 3, 0)
    wim = _np.asarray(L1_conv_weight_im).transpose(1, 2, 3, 0)
    p_w = _np.zeros((2, C, SLOTS, 2, C), _np.float32)
    q_w = _np.zeros((2, C, SLOTS, 2, C), _np.float32)
    for n, (k, l, cplx) in enumerate(frequency_slots()):
        for lane, f in enumerate((k, l)):
            m = ((-f[0]) % N_FREQ, (-f[1]) % N_FREQ)
            p_w[lane, :, n, lane], q_w[lane, :, n, lane] = wre[:, f[0], f[1]], wre[:, m[0], m[1]]
            if cplx:
                a, b = wim[:, f[0], f[1]], wim[:, m[0], m[1]]
                p_w[lane, :, n, 1 - lane], q_w[lane, :, n, 1 - lane] = (a, b) if lane == 0 else (b, a)
    arrays = {
        "x": x, "p_w": p_w.reshape(P, SLOTS, P), "q_w": q_w.reshape(P, SLOTS, P), "cw0": cw0.reshape(P, P),
        "cw1": cw1.reshape(P, P), "w_mix": mix.reshape(P, 2 * K0 * C),
        "conv_b": _np.asarray(L0_conv_conv_b).reshape(1, C), "bias": _np.asarray(L0_conv_bias).reshape(1, 1),
    }
    tables = constants()
    for name in ("ident", "ident16", "gmean", "fwd", "inv", "dft", "taps", "rows", "cols"):
        arrays["c_" + name] = tables[name]
    nc = _bacc.Bacc("TRN2", target_bir_lowering=False, num_devices=1)
    args, given = [], {}
    for name, a in arrays.items():
        a = _np.ascontiguousarray(a)
        given[f"in_{name}_dram"] = a
        args.append(nc.dram_tensor(f"in_{name}_dram", a.shape, _mybir.dt.from_np(a.dtype), kind="ExternalInput").ap())
    args.append(nc.dram_tensor(_OUT, x.shape, _mybir.dt.float32, kind="ExternalOutput").ap())
    nc.disable_value_cache = True
    conv_preact_kernel(nc, *args)
    r = _run(nc, [given], core_ids=[0])
    return r.results[0][_OUT]
```

```python
import math

import numpy as np
import concourse.bass as bass
from concourse import mybir
from contextlib import ExitStack

C, H, W = 64, 128, 128
P = 128
GROUPS = 32
EPS = 1e-5
K0 = 3
TRUNC = 16
M_TILE, N_FREQ = 8, 10
TILES = H // M_TILE
PX = N_FREQ * N_FREQ
SLOTS = PX // 2

HALF = H // 2
ROWPAIRS = H // 2
BLOCKS = ROWPAIRS + 1
GCHUNK = 4
GCHUNKS = -(-BLOCKS // GCHUNK)
CONV_FILLS = ROWPAIRS // 4
PAIRS = TILES * TILES // 2
GRP = 2
T1_FILLS = PAIRS // GRP // 4
FW_FILLS = T1_FILLS // 2
FQ_FILLS = -(-SLOTS // 4)
T2_FILLS = C // 4
IN_FILLS = PAIRS // GRP // 8
KEPT = M_TILE * M_TILE
SPEC_SCALE = 32.0
BOX_ORDER = list(range(-(-SLOTS // GCHUNK), GCHUNKS)) + list(range(-(-SLOTS // GCHUNK)))


def transform_matrices(inverse):
    n, sign = N_FREQ, 1.0 if inverse else -1.0
    k = np.arange(n)[:, None]
    i = np.arange(n)[None, :]
    ang = sign * 2.0 * np.pi * k * i / n
    ang = (ang + np.pi) % (2.0 * np.pi) - np.pi
    neg = np.zeros((n, n), dtype=bool)
    hi = ang > np.pi / 2
    ang = np.where(hi, ang - np.pi, ang)
    neg |= hi
    lo = ang < -np.pi / 2
    ang = np.where(lo, ang + np.pi, ang)
    neg |= lo
    size = float(2 ** 20)
    lam = np.round(-np.tan(ang / 2.0) * size) / size
    gam = np.round(np.sin(ang) * size) / size
    s = np.where(neg, -1.0, 1.0)
    out = (s * (1.0 + lam * gam), s * (2.0 * lam + gam * lam * lam), s * gam, s * (1.0 + gam * lam))
    return [m.astype(np.float32).astype(np.float64) for m in out]


def frequency_slots():
    slots, seen = [], set()
    for a in range(N_FREQ):
        for b in range(N_FREQ):
            partner = ((-a) % N_FREQ, (-b) % N_FREQ)
            if (a, b) != partner and partner not in seen:
                seen.add((a, b))
                slots.append(((a, b), (a, b), True))
    h = N_FREQ // 2
    slots.append(((0, 0), (0, h), False))
    slots.append(((h, 0), (h, h), False))
    return slots


def constants():
    f32 = np.float32
    out = {}
    out["ident"] = np.eye(P, dtype=f32)
    out["ident16"] = np.eye(P, dtype=np.float16)
    grp = (np.arange(P) % C) // (C // GROUPS)
    out["gmean"] = (grp[:, None] == grp[None, :]).astype(f32) / (2 * C // GROUPS)
    rr, ri, ir, ii = transform_matrices(False)
    re = np.einsum("bj,ai->ijab", rr, rr) + np.einsum("bj,ai->ijab", ir, ri)
    im = np.einsum("bj,ai->ijab", rr, ir) + np.einsum("bj,ai->ijab", ir, ii)
    fwd = np.zeros((P, 2, SLOTS))
    slots = frequency_slots()
    for n, (k, l, cplx) in enumerate(slots):
        fwd[:PX, 0, n] = re[:, :, k[0], k[1]].reshape(-1)
        fwd[:PX, 1, n] = (im if cplx else re)[:, :, l[0], l[1]].reshape(-1)
    out["fwd"] = (fwd.reshape(P, PX) / SPEC_SCALE).astype(f32)
    rr, ri, ir, ii = transform_matrices(True)
    sc = 1.0 / N_FREQ ** 2
    are = (np.einsum("jb,ia->abij", rr, rr) + np.einsum("jb,ia->abij", ir, ri)) * sc
    aim = (np.einsum("jb,ia->abij", ri, rr) + np.einsum("jb,ia->abij", ii, ri)) * sc
    inv = np.zeros((P, KEPT))
    for n, (k, l, cplx) in enumerate(slots):
        a = are[k[0], k[1], 1:1 + M_TILE, 1:1 + M_TILE].reshape(-1)
        b = (aim if cplx else are)[l[0], l[1], 1:1 + M_TILE, 1:1 + M_TILE].reshape(-1)
        half = 1.0 if cplx else 0.5
        inv[2 * n], inv[2 * n + 1] = half * a, half * b
    inv = (inv * SPEC_SCALE).astype(f32)
    hi = inv.astype(np.float16)
    out["inv"] = np.concatenate([hi, (inv - hi.astype(f32)).astype(np.float16)], 1)
    th = 2 * np.pi / H
    pos, kk = np.arange(H), np.arange(TRUNC)
    e = np.exp(-1j * th * pos[:, None] * kk[None, :])
    out["dft"] = np.stack([e.real, e.imag], -1).reshape(H, 2 * TRUNC).astype(f32)
    r = np.zeros((2, K0, TRUNC, 4, 2, 4, TRUNC, 2))
    for rih in range(2):
        for a in range(K0):
            for kx in range(TRUNC):
                for riw in range(2):
                    z = (1j ** (rih + riw)) * np.exp(-1j * th * a * kx)
                    for q in range(4):
                        r[rih, a, kx, q, riw, q, kx, 0] = z.real
                        r[rih, a, kx, q, riw, q, kx, 1] = z.imag
    out["taps"] = r.reshape(2 * K0, P, P).transpose(1, 0, 2).reshape(P, 2 * K0 * P).astype(f32)
    g = np.zeros((4, 2, 4, TRUNC, 2, H))
    ph = np.exp(1j * th * kk[:, None] * pos[None, :]) / (H * W)
    for q in range(4):
        g[q, 0, q, :, 0], g[q, 0, q, :, 1] = ph.real, -ph.imag
        g[q, 1, q, :, 0], g[q, 1, q, :, 1] = ph.imag, ph.real
    out["rows"] = g.reshape(8, P, H).transpose(1, 0, 2).reshape(P, 8 * H).astype(f32)
    box = sum(np.exp(-1j * th * b * kk) for b in range(K0))
    d = box[:, None] * np.exp(1j * th * kk[:, None] * pos[None, :])
    base = np.stack([d.real, -d.imag], 1).reshape(2 * TRUNC, W)
    hi = base.astype(np.float16)
    lo = (base - hi.astype(np.float64)).astype(np.float16)
    out["cols"] = np.concatenate([hi, lo, hi, lo], 0)
    return out


def conv_preact_kernel(nc, x, p_w, q_w, cw0, cw1, w_mix, conv_b, bias, c_ident, c_ident16, c_gmean, c_fwd,
                       c_inv, c_dft, c_taps, c_rows, c_cols, out):
    f32, f16 = mybir.dt.float32, mybir.dt.float16
    ALU = mybir.AluOpType
    ACT = mybir.ActivationFunctionType
    B = x.shape[0]
    U = 2
    TRIPS = B // U
    x_v = x.rearrange("(n u) c h w -> n u c h w", u=U)
    out_v = out.rearrange("(n u) c h w -> n u c h w", u=U)

    ctx = ExitStack()
    with ctx:
        def sb(name, shape, dt=f32):
            return ctx.enter_context(nc.sbuf_tensor(name, shape, dt))

        def sem(name):
            return ctx.enter_context(nc.semaphore(name))

        xr = [sb(f"xr{u}", [P, HALF, W]) for u in range(U)]
        xh = [sb(f"xh{r}", [P, 4, W])[:, :, :] for r in range(3)]
        g = [sb(f"g{r}", [P, GCHUNK, W + 2]) for r in range(2)]
        s_x = sb("s_x", [P, BLOCKS * W])
        s = s_x[:, :].rearrange("p (r w) -> p r w", w=W)
        spec = s_x[:, 0:SLOTS * P].rearrange("p (f t) -> p f t", t=P)
        tb = [s_x[:, SLOTS * P + 8 * PX * r:SLOTS * P + 8 * PX * (r + 1)] for r in range(2)]
        u2 = sb("u2", [P, (HALF + 2) * (W + 2)])
        xn = u2[:, :].rearrange("p (r w) -> p r w", w=W + 2)
        qt = [u2[:, C * P // 2 * v:C * P // 2 * (v + 1)].bitcast(f16).rearrange("p (t h o) -> p t h o", h=2, o=C)
              for v in range(2)]
        ft = u2[:, 0:C * H // 2].bitcast(f16).rearrange("p (h o) -> p h o", o=C)
        q_in = u2[:, 0:SLOTS * P].rearrange("p (f o) -> p f o", o=P)
        wf = sb("wf", [P, SLOTS, P])
        u3 = sb("u3", [P, PX * C])
        yt = u3[:, :].rearrange("p (o k) -> p o k", k=PX)
        a_t = u3[:, 0:2048].rearrange("p (j n) -> p j n", j=4)
        b_t = u3[:, 2048:4096].rearrange("p (k c) -> p k c", c=C)
        g16 = u3[:, 0:4096].bitcast(f16).rearrange("p (o v k) -> p o v k", v=4, k=2 * TRUNC)
        u_t = xh[2][:, :, :].rearrange("p q (kx n) -> p q kx n", n=8)
        y_t = u3[:, 4608:6144].rearrange("p (q n) -> p q n", q=4)
        z_t = u3[:, 6144:6400]
        xh.append(u3[:, 4608:5120].rearrange("p (c w) -> p c w", w=W))
        px = [sb(f"px{r}", [P, 4 * P]) for r in range(2)]
        ident, ident16 = sb("ident", [P, P]), sb("ident16", [P, P], f16)
        gmean, fwd, inv = sb("gmean", [P, P]), sb("fwd", [P, PX]), sb("inv", [P, 2 * KEPT], f16)
        dft, taps, rows = sb("dft", [P, 2 * TRUNC]), sb("taps", [P, 2 * K0, P]), sb("rows", [P, 8, H])
        cols = sb("cols", [P, W], f16)
        w0, w1, wm = sb("w0", [P, P]), sb("w1", [P, P]), sb("wm", [P, 2 * K0 * C])
        brow, b1 = sb("brow", [1, C]), sb("b1", [1, 1])
        st = sb("st", [P, HALF // 4, 6])
        sm = [sb(f"sm{n}", [P, 12]) for n in range(2)]
        dcs = sb("dcs", [P, 1])
        carry = sb("carry", [P, 3])

        ps = [ctx.enter_context(nc.psum_tensor(f"ps{b}", [P, 512], f32)) for b in range(4)]
        pw = [ctx.enter_context(nc.psum_tensor(f"pw{b}", [P, 2, 512], f32)) for b in range(2)]
        wide = [pw[b // 2][:, b % 2, :] for b in range(4)]

        const_in, weight_in, weight_done = sem("const_in"), sem("weight_in"), sem("weight_done")
        pads_set = sem("pads_set")
        x_in = [sem(f"x_in{u}") for u in range(U)]
        xh_in = [sem(f"xh_in{r}") for r in range(4)]
        x_out = [sem(f"x_out{u}") for u in range(U)]
        xh_read = sem("xh_read")
        vec_step = sem("vec_step")
        stat_ready = sem("stat_ready")
        stat_mean = sem("stat_mean")
        v_ready, sd_ready = sem("v_ready"), sem("sd_ready")
        norm_ready = sem("norm_ready")
        pool_step = sem("pool_step")
        g_used = sem("g_used")
        a_done = sem("a_done")
        b_full, b_done = sem("b_full"), sem("b_done")
        uu_full, uu_out, uu_done = sem("uu_full"), sem("uu_out"), sem("uu_done")
        y_full, y_done = sem("y_full"), sem("y_done")
        z_full, z_done = sem("z_full"), sem("z_done")
        gg_full, hi_done, lo_done = sem("gg_full"), sem("hi_done"), sem("lo_done")
        dup_done = sem("dup_done")
        ft_full = sem("ft_full")
        ft_even, ft_odd = sem("ft_even"), sem("ft_odd")
        conv_full, conv_done = sem("conv_full"), sem("conv_done")
        xn_ready = sem("xn_ready")
        tb_ready = sem("tb_ready")
        t1_full, t1_done = sem("t1_full"), sem("t1_done")
        px_used = sem("px_used")
        fw_even, fw_odd_upper, fw_odd_lower = sem("fw_even"), sem("fw_odd_upper"), sem("fw_odd_lower")
        fq_full, fq_done = sem("fq_full"), sem("fq_done")
        t2_full = sem("t2_full")
        t2_high, t2_low = sem("t2_high"), sem("t2_low")
        in_full, in_done = sem("in_full"), sem("in_done")

        T1_ALL, FW_ALL, FQ_ALL = GRP * T1_FILLS, GRP * FW_FILLS, GRP * FQ_FILLS
        TB_ALL = T1_ALL // 2
        T2_ALL, IN_ALL = GRP * T2_FILLS, GRP * IN_FILLS
        XH_CHUNKS = C // 4
        BANDS = [M_TILE + 1, 3 * M_TILE + 1, 5 * M_TILE + 1, HALF]
        FT_BANKS = [2, 3, 0, 1, 2, 3, 2, 3]
        LAST = TRIPS - 1

        def upto(it, u, per_image, k=0):
            return it * (U * per_image) + (u * per_image + k)

        def windows(row, col):
            return bass.AP(tensor=u2[:, :].tensor, offset=row * (W + 2) + col,
                           ap=[[(HALF + 2) * (W + 2), P], [M_TILE, 8], [W + 2, N_FREQ], [1, N_FREQ]])

        def apart(eng, h=0):
            if eng is nc.gpsimd:
                col = carry[C * h:C * h + 16, :]
                eng.tensor_tensor(col[:, 0:1], col[:, 2:3], col[:, 2:3], ALU.add)
            else:
                eng.tensor_copy(carry[:, 1:2], carry[:, 2:3])

        def trips(eng, image):
            if LAST > 0:
                with eng.Fori(0, LAST) as it:
                    for u in range(U):
                        image(it, u, True)
            image(LAST, 0, True)
            image(LAST, 1, False)

        block = ctx.enter_context(nc.Block())

        @block.sync
        def _(sp):
            def rows_of_channels(it, u, first):
                for n in range(XH_CHUNKS):
                    if n >= 4:
                        sp.wait_ge(xh_read, upto(it, u, XH_CHUNKS, n - 3))
                    elif n == 3 and not first:
                        sp.wait_ge(z_full, upto(it, u, 1))
                    elif n == 2 and not first:
                        sp.wait_ge(y_full, upto(it, u, 4))
                    elif not first:
                        sp.wait_ge(xh_read, upto(it, u, XH_CHUNKS))
                    sp.dma_start(xh[n % 4][:, :, :], x_v[it, u, 4 * n:4 * n + 4, :, :].rearrange("c h w -> h c w")
                                 ).then_inc(xh_in[n % 4], 16)

            def halves(it, u):
                for h in range(2):
                    sp.dma_start(xr[u][C * h:C * h + C, :, :],
                                 x_v[it, u, :, HALF * h:HALF * h + HALF, :]).then_inc(x_in[u], 16)

            halves(0, 0)
            rows_of_channels(0, 0, True)
            rows_of_channels(0, 1, False)
            halves(0, 1)
            if LAST > 0:
                with sp.Fori(1, TRIPS) as it:
                    for u in range(U):
                        rows_of_channels(it, u, False)
                        sp.wait_ge(x_out[u], it * 64)
                        halves(it, u)

        def staggered(n):
            pieces = []
            for par in range(2):
                j, nb = 0, min(GCHUNK, BLOCKS - GCHUNK * n)
                while j < nb:
                    row = 2 * (GCHUNK * n + j) - 1 + par
                    cnt = 1
                    if 0 <= row < H:
                        while j + cnt < nb and row + 2 * cnt < H and (row + 2 * cnt) // HALF == row // HALF:
                            cnt += 1
                        pieces.append((par, j, cnt, row // HALF, row % HALF))
                    else:
                        pieces.append((par, j, cnt, None, None))
                    j += cnt
            return pieces

        POOL_SUMS = 14

        def steps_to(n):
            return sum(len(staggered(m)) for m in BOX_ORDER[:n + 1]) + min(n + 1, POOL_SUMS)

        BOX_STEPS = steps_to(GCHUNKS)
        POOL = BOX_STEPS + len(BANDS) - 1

        def input_chunk(n, u):
            chunk = BOX_ORDER[n]
            nb = min(GCHUNK, BLOCKS - GCHUNK * chunk)
            return s[:, GCHUNK * chunk:GCHUNK * chunk + nb, :], g[(u * GCHUNKS + n) % 2][:, 0:nb, :]

        @block.gpsimd
        def _(pool):
            def normalise(it, u, first):
                x1, steps = xr[u % U], 0
                pool.wait_ge(norm_ready, upto(it, u, 2, 1))
                for n, chunk in enumerate(BOX_ORDER):
                    k = u * GCHUNKS + n
                    if k >= 2:
                        pool.wait_ge(g_used, upto(it, u, GCHUNKS, n - 1))
                    for par, j, cnt, h, lr in staggered(chunk):
                        if k or steps:
                            pool.wait_ge(pool_step, upto(it, u, POOL, steps))
                        apart(pool, par if h is None else h)
                        dst = g[k % 2][C * par:C * par + C, j:j + cnt, 1:W + 1]
                        if h is None:
                            pool.memset(dst, 0.0).then_inc(pool_step, 1)
                        else:
                            pool.tensor_scalar(dst, x1[C * h:C * h + C, lr:lr + 2 * cnt - 1:2, :],
                                               sm[0][C * h:C * h + C, 6:7], sm[0][C * h:C * h + C, 8:9],
                                               ALU.mult, ALU.add).then_inc(pool_step, 1)
                        steps += 1
                    if n >= POOL_SUMS:
                        continue
                    if n == 0 and not first:
                        pool.wait_ge(t1_full, upto(it, u - 1, T1_ALL, T1_ALL))
                    if chunk < FQ_FILLS and not first:
                        pool.wait_ge(fq_full, upto(it, u - 1, FQ_ALL, FQ_FILLS + chunk + 1))
                    pool.wait_ge(pool_step, upto(it, u, POOL, steps))
                    dst, src = input_chunk(n, u)
                    pool.tensor_tensor(dst, src[:, :, 0:W], src[:, :, 1:W + 1], ALU.add).then_inc(pool_step, 1)
                    steps += 1

            def bands(it, u):
                pool.wait_ge(norm_ready, upto(it, u, 2, 2))
                for b in range(1, len(BANDS)):
                    top, end = BANDS[b - 1], BANDS[b]
                    pool.wait_ge(pool_step, upto(it, u, POOL, BOX_STEPS + b - 1))
                    apart(pool)
                    pool.tensor_scalar(xn[:, top + 1:end + 1, 1:W + 1], xr[u][:, top:end, :],
                                       sm[1][:, 6:7], sm[1][:, 8:9], ALU.mult, ALU.add).then_inc(pool_step, 1)

            def store(it, u, grp):
                pool.wait_ge(in_done, upto(it, u, IN_ALL, (grp + 1) * IN_FILLS))
                for h in range(2):
                    lr = grp * HALF // 2
                    pool.dma_start(out_v[it, u, :, HALF * h + lr:HALF * h + lr + HALF // 2, :],
                                   xr[u][C * h:C * h + C, lr:lr + HALF // 2, :]).then_inc(x_out[u], 16)

            def image(it, u, more):
                bands(it, u)
                if more:
                    normalise(it, u + 1, False)
                store(it, u, 0)
                store(it, u, 1)

            pool.wait_ge(pads_set, 1)
            pool.wait_ge(x_in[0], 32)
            pool.dma_start(wf[:, :, :], p_w).then_inc(weight_in, 16)
            pool.dma_start(q_in, q_w).then_inc(weight_in, 16)
            normalise(0, 0, True)
            trips(pool, image)
            for u in range(U):
                pool.wait_ge(x_out[u], 64 * TRIPS)

        VEC = 2 * (1 + 1 + 4) + 1 + 1 + GCHUNKS - POOL_SUMS

        @block.vector
        def _(dve):
            chain = [0]
            where = [0, 0]

            def link(ins):
                chain[0] += 1
                ins.then_inc(vec_step, 1)
                dve.wait_ge(vec_step, where[0] * (U * VEC) + where[1] + chain[0])

            def rowstats(x1, m):
                return dve.bn_stats(st[:, m, :], x1[:, 4 * m:4 * m + 4, :].rearrange("p r w -> p (r w)"))

            def average(n, last):
                link(last)
                apart(dve)
                dve.bn_aggr(sm[n][:, 0:2], st[:, :, :]).then_inc(stat_ready, 1)

            def spread(it, u, n):
                m = sm[n]
                dve.wait_ge(stat_mean, upto(it, u, 4, 2 * n + 1))
                dve.tensor_copy(m[:, 9:10], ps[1][:, 0:1])
                link(dve.tensor_tensor(m[:, 2:3], m[:, 0:1], ps[1][:, 0:1], ALU.subtract))
                dve.scalar_tensor_tensor(m[:, 3:4], m[:, 2:3], m[:, 2:3], m[:, 1:2],
                                         ALU.mult, ALU.add).then_inc(stat_ready, 1)

            def variance(it, u, n):
                dve.wait_ge(stat_mean, upto(it, u, 4, 2 * n + 2))
                dve.tensor_scalar(sm[n][:, 4:5], ps[0][:, 0:1], EPS, None, ALU.add).then_inc(v_ready, 1)

            def scale(it, u, n):
                m = sm[n]
                dve.wait_ge(sd_ready, upto(it, u, 2, n + 1))
                link(dve.reciprocal(m[:, 6:7], m[:, 5:6]))
                link(dve.tensor_scalar(m[:, 7:8], m[:, 6:7], m[:, 6:7], m[:, 4:5], ALU.mult, ALU.mult))
                link(dve.tensor_scalar(m[:, 7:8], m[:, 7:8], -0.5, 1.5, ALU.mult, ALU.add))
                link(dve.tensor_scalar(m[:, 6:7], m[:, 6:7], m[:, 7:8], None, ALU.mult))
                return dve.tensor_scalar(m[:, 8:9], m[:, 9:10], m[:, 6:7], -1.0, ALU.mult, ALU.mult)

            def statistics(it, u):
                dve.wait_ge(x_in[u % U], it * 32 + 32 * (1 + u // U))
                for m in range(HALF // 4):
                    last = rowstats(xr[u % U], m)
                average(0, last)

            def constant_term(it, u):
                link(scale(it, u, 0))
                dve.tensor_scalar(dcs[0:C, :], sm[0][0:C, 8:9], float(H * W), None, ALU.mult).then_inc(norm_ready, 1)

            def box(it, u, n):
                dve.wait_ge(pool_step, upto(it, u, POOL, steps_to(n)))
                dst, src = input_chunk(n, u)
                if n >= POOL_SUMS:
                    link(dve.tensor_tensor(dst, src[:, :, 0:W], src[:, :, 1:W + 1], ALU.add))
                dve.tensor_tensor(dst, dst, src[:, :, 2:W + 2], ALU.add).then_inc(g_used, 1)

            def summed(it, u):
                dve.wait_ge(z_full, upto(it, u, 1, 1))
                link(dve.tensor_copy(z_t, wide[0][:, 0:4 * C]))
                dve.tensor_tensor(z_t[0:1, 0:C], z_t[0:1, 0:C], brow[:, :], ALU.add).then_inc(z_done, 1)

            def low_parts(it, u):
                for q in range(4):
                    dve.wait_ge(hi_done, upto(it, u, 4, q + 1))
                    dst = g16.rearrange("p o v (kg q r) -> p v q r kg o", q=4, r=2)
                    src = wide[q].rearrange("p (r kg o) -> p r kg o", r=2, kg=4)
                    dve.tensor_tensor(dst[:, 2, q, :], src, dst[:, 0, q, :], ALU.subtract).then_inc(lo_done, 1)

            def coefficients(it, u):
                for n in range(0, 8, 2):
                    dve.wait_ge(ft_full, upto(it, u, 8, n + 1))
                    dve.tensor_copy(ft[:, :, 8 * n:8 * n + 8].rearrange("p h o -> p o h"),
                                    ps[FT_BANKS[n]][:, :].bitcast(f16).rearrange("p (o h) -> p o h", h=H)
                                    ).then_inc(ft_even, 1)

            def convolved(it, u):
                for n in range(CONV_FILLS):
                    h, j = n % 2, n // 2
                    dve.wait_ge(conv_full, upto(it, u, CONV_FILLS, n + 1))
                    for par in range(2):
                        dst = xr[u][C * h:C * h + C, 8 * j + par:8 * j + 8:2, :]
                        ins = dve.tensor_tensor(dst, ps[n % 2][C * par:C * par + C, :].rearrange("p (r w) -> p r w", w=W),
                                                dst, ALU.add)
                    ins.then_inc(conv_done, 1)
                    if h == 0 and j:
                        dve.wait_ge(conv_done, upto(it, u, CONV_FILLS, n))
                        rowstats(xr[u], 2 * j - 2)
                        rowstats(xr[u], 2 * j - 1)
                dve.wait_ge(conv_done, upto(it, u, CONV_FILLS, CONV_FILLS))
                rowstats(xr[u], 14)
                average(1, rowstats(xr[u], 15))
                dve.memset(xn[:, :, 0:1], 0.0)
                dve.memset(xn[:, :, W + 1:W + 2], 0.0)
                dve.memset(xn[0:C, 0:1, 1:W + 1], 0.0)
                dve.memset(xn[C:P, HALF + 1:HALF + 2, 1:W + 1], 0.0)
                spread(it, u, 1)
                variance(it, u, 1)
                scale(it, u, 1).then_inc(norm_ready, 1)

            def gather(it, u, n):
                th, tw = 8 * n // TILES, 8 * n % TILES
                if n >= 2:
                    dve.wait_ge(t1_full, upto(it, u, T1_ALL, 2 * (n - 1)))
                last = th == HALF // M_TILE - 1
                dve.wait_ge(xn_ready, upto(it, u, 2, 2 if last else 1))
                need = min(HALF, M_TILE * th + M_TILE + 1)
                band = min(b for b in range(len(BANDS)) if BANDS[b] >= need)
                if band:
                    dve.wait_ge(pool_step, upto(it, u, POOL, BOX_STEPS + band))
                dve.tensor_copy(tb[n % 2].rearrange("p (t y x) -> p t y x", t=8, y=N_FREQ),
                                windows(M_TILE * th, M_TILE * tw)).then_inc(tb_ready, 1)

            def spectra(it, u, grp, more):
                for n in range(FW_FILLS):
                    k = grp * FW_FILLS + n
                    if more and grp and n == 2:
                        constant_term(it, u + 1)
                    if k + 2 < TB_ALL:
                        gather(it, u, k + 2)
                    dve.wait_ge(px_used, upto(it, u, T1_ALL, 2 * (k + 1)))
                    if n == 0 and grp > 0:
                        dve.wait_ge(fq_full, upto(it, u, FQ_ALL, grp * FQ_FILLS))
                    for h in ((1,) if n % 2 else (0, 1)):
                        src = pw[n % 2][C * h:C * h + C, :, 0:4 * PX].rearrange("p b (t v f) -> p v f b t", v=2, f=SLOTS)
                        for v in range(2):
                            dst = spec[C * v:C * v + C, :, 64 * h + 8 * n:64 * h + 8 * n + 8].rearrange("p f (b t) -> p f b t", b=2)
                            ins = dve.tensor_copy(dst, src[:, v])
                    ins.then_inc(fw_odd_upper if n % 2 else fw_even, 1)
                    if more and grp and n == 0:
                        variance(it, u + 1, 0)

            def transposed(it, u, grp, after):
                for n in range(T2_FILLS):
                    k = grp * T2_FILLS + n
                    dve.wait_ge(t2_high, upto(it, u, T2_ALL, k + 1))
                    high, low = (qt[v][0:PX, :, :, 4 * n:4 * n + 4].rearrange("p t h o -> p o h t") for v in range(2))
                    dve.tensor_tensor(low, ps[(n + 2) % 4][0:PX, :].rearrange("p (o h t) -> p o h t", o=4, h=2), high,
                                      ALU.subtract).then_inc(t2_low, 1)
                    if n in after:
                        box(it, u + 1, after[n])

            def result(it, u, grp, n):
                dve.wait_ge(in_full, upto(it, u, IN_ALL, grp * IN_FILLS + n + 1))
                th, tw = (grp * 64 + 8 * n) // TILES, (8 * n) % TILES
                dst = xr[u][:, M_TILE * th:M_TILE * th + M_TILE, M_TILE * tw:M_TILE * tw + 64].rearrange(
                    "p y (t x) -> p t y x", t=8)
                src = ps[n % 2][:, :].rearrange("p (t y x) -> p t y x", t=8, y=M_TILE)
                dve.tensor_tensor(dst, src, dst, ALU.add).then_inc(in_done, 1)

            def image(it, u, more):
                where[0], where[1], chain[0] = it, (u + 1) * VEC, 0
                coefficients(it, u)
                convolved(it, u)
                gather(it, u, 0)
                gather(it, u, 1)
                spectra(it, u, 0, more)
                if more:
                    statistics(it, u + 1)
                    spread(it, u + 1, 0)
                spectra(it, u, 1, more)
                transposed(it, u, 0, {1: 0, 6: 1, 11: 2, 15: 3} if more else {})
                if more:
                    for n in (4,):
                        box(it, u + 1, n)
                boxes = {1: 5, 3: 6, 5: 7, 7: 8} if more else {}
                for n in range(IN_FILLS):
                    result(it, u, 0, n)
                    if n in boxes:
                        box(it, u + 1, boxes[n])
                transposed(it, u, 1, {3: 9, 8: 10, 13: 11} if more else {})
                boxes = {1: (12,), 3: (13,), 5: (14,), 6: (15,), 7: (16,)}
                for n in range(IN_FILLS):
                    if more and n == 2:
                        summed(it, u + 1)
                    if more and n == 4:
                        low_parts(it, u + 1)
                    result(it, u, 1, n)
                    for m in boxes.get(n, ()) if more else ():
                        box(it, u + 1, m)
                assert not more or chain[0] == VEC, chain[0]

            for r in range(2):
                dve.memset(g[r][:, :, 0:1], 0.0)
                dve.memset(g[r][:, :, W + 1:W + 2], 0.0)
                dve.memset(px[r][96:P, :], 0.0)
            dve.memset(carry[:, :], 0.0)
            dve.memset(dcs[:, :], 0.0).then_inc(pads_set, 1)
            dve.wait_ge(pads_set, 1)
            statistics(0, 0)
            spread(0, 0, 0)
            variance(0, 0, 0)
            constant_term(0, 0)
            blocks = ((0, 0, ALU.add), (C, C, ALU.add), (0, C, ALU.subtract), (C, 0, ALU.subtract))
            for n in range(GCHUNKS):
                box(0, 0, n)
                if n == 8:
                    dve.wait_ge(weight_in, 32)
                if 8 <= n < 12:
                    lo_p, lo_c, op = blocks[n - 8]
                    blk = wf[lo_p:lo_p + C, :, lo_c:lo_c + C]
                    dve.tensor_tensor(blk, blk, q_in[lo_p:lo_p + C, :, lo_c:lo_c + C], op).then_inc(weight_done, 1)
            dve.wait_ge(const_in, 16 * 14)
            link(dve.tensor_scalar(brow[:, :], brow[:, :], b1[:, :], float(H * W) / K0, ALU.add, ALU.mult))
            summed(0, 0)
            low_parts(0, 0)
            dve.wait_ge(weight_done, 4)
            dve.engine_nop().then_inc(vec_step, VEC - chain[0])
            trips(dve, image)

        @block.scalar
        def _(act):
            def root(it, u, n):
                act.wait_ge(v_ready, upto(it, u, 2, n + 1))
                act.activation(sm[n][:, 5:6], sm[n][:, 4:5], ACT.Sqrt).then_inc(sd_ready, 1)

            def rows_dft(it, u):
                def out(q):
                    act.wait_ge(xh_read, upto(it, u, XH_CHUNKS, 4 * (q + 1)))
                    act.copy(a_t[:, q, :], wide[q]).then_inc(a_done, 1)

                def transposed_out(q):
                    act.wait_ge(b_full, upto(it, u, 4, q + 1))
                    dst = b_t[:, :, 16 * q:16 * q + 16].rearrange("p k (g cc) -> p cc g k", cc=4)
                    src = ps[2 + q % 2][:, :].rearrange("p (cc g k) -> p cc g k", cc=4, g=4)
                    act.copy(dst, src).then_inc(b_done, 1)

                for q in range(3):
                    out(q)
                for q in range(3):
                    transposed_out(q)
                out(3)
                transposed_out(3)

            def spectrum(it, u):
                act.wait_ge(uu_full, upto(it, u, 1, 1))
                act.copy(u_t, wide[0].rearrange("p (kx q n) -> p q kx n", q=4, n=8)).then_inc(uu_out, 1)

            def spectrum_normalised(it, u):
                act.wait_ge(norm_ready, upto(it, u, 2, 1))
                act.wait_ge(uu_out, upto(it, u, 1, 1))
                act.activation(u_t, u_t, ACT.Copy, scale=sm[0][:, 6:7]).then_inc(uu_done, 1)
                act.wait_ge(uu_done, upto(it, u, 2, 1))
                act.activation(u_t[:, 0, 0, 0:1], u_t[:, 0, 0, 0:1], ACT.Identity, bias=dcs[:, :]).then_inc(uu_done, 1)

            def mixed(it, u):
                for q in range(4):
                    act.wait_ge(y_full, upto(it, u, 4, q + 1))
                    act.copy(y_t[:, q, :], wide[q][:, 0:2 * K0 * C]).then_inc(y_done, 1)

            def high_parts(it, u):
                dst = g16.rearrange("p o v (kg q r) -> p v q r kg o", q=4, r=2)
                for q in range(4):
                    act.wait_ge(gg_full, upto(it, u, 4, q + 1))
                    src = wide[q].rearrange("p (r kg o) -> p r kg o", r=2, kg=4)
                    act.copy(dst[:, 0, q, :], src).then_inc(hi_done, 1)
                act.wait_ge(hi_done, upto(it, u, 4, 4))
                act.copy(g16[:, :, 1, :], g16[:, :, 0, :])
                act.wait_ge(lo_done, upto(it, u, 4, 4))
                act.copy(g16[:, :, 3, :], g16[:, :, 2, :]).then_inc(dup_done, 1)

            def normalised(it, u):
                act.wait_ge(norm_ready, upto(it, u, 2, 2))
                sc, sh = sm[1][:, 6:7], sm[1][:, 8:9]
                act.activation(xn[C:P, 0, 1:W + 1], xr[u][0:C, HALF - 1, :], ACT.Identity, bias=sh[0:C], scale=sc[0:C])
                act.activation(xn[:, 1:BANDS[0] + 1, 1:W + 1], xr[u][:, 0:BANDS[0], :], ACT.Identity, bias=sh, scale=sc
                               ).then_inc(xn_ready, 1)
                act.activation(xn[0:C, HALF + 1, 1:W + 1], xr[u][C:P, 0, :], ACT.Identity, bias=sh[C:P],
                               scale=sc[C:P]).then_inc(xn_ready, 1)

            def coefficients(it, u):
                for n in range(1, 8, 2):
                    act.wait_ge(ft_full, upto(it, u, 8, n + 1))
                    act.copy(ft[:, :, 8 * n:8 * n + 8].rearrange("p h o -> p o h"),
                             ps[FT_BANKS[n]][:, :].bitcast(f16).rearrange("p (o h) -> p o h", h=H)).then_inc(ft_odd, 1)

            def pixels_and_spectra(it, u, grp, more):
                for n in range(T1_FILLS + 1):
                    if more and grp and n == 5:
                        root(it, u + 1, 0)
                    if n < T1_FILLS:
                        k = grp * T1_FILLS + n
                        act.wait_ge(t1_full, upto(it, u, T1_ALL, k + 1))
                        if k >= 2:
                            act.wait_ge(px_used, upto(it, u, T1_ALL, k - 1))
                        act.copy(px[n % 2][0:PX, :], ps[2 + n % 2][0:PX, :]).then_inc(t1_done, 1)
                    if n < 4:
                        continue
                    m = (n // 4) * 2 - 1
                    k = grp * FW_FILLS + m
                    if n % 4 == 0:
                        act.wait_ge(px_used, upto(it, u, T1_ALL, 2 * (k + 1)))
                        if m == 1 and grp > 0:
                            act.wait_ge(fq_full, upto(it, u, FQ_ALL, grp * FQ_FILLS))
                    for v in (range(2) if n == T1_FILLS else range(n % 4, n % 4 + 1) if n % 4 < 2 else ()):
                        src = pw[1][0:C, :, 0:4 * PX].rearrange("p b (t v f) -> p v f b t", v=2, f=SLOTS)
                        dst = spec[C * v:C * v + C, :, 8 * m:8 * m + 8].rearrange("p f (b t) -> p f b t", b=2)
                        ins = act.copy(dst, src[:, v])
                        if v == 1:
                            ins.then_inc(fw_odd_lower, 1)

            def products(it, u, grp):
                for n in range(FQ_FILLS):
                    k = grp * FQ_FILLS + n
                    nf = min(4, SLOTS - 4 * n)
                    act.wait_ge(fq_full, upto(it, u, FQ_ALL, k + 1))
                    if n == 0:
                        if grp:
                            act.wait_ge(t2_full, upto(it, u, T2_ALL, grp * T2_FILLS))
                        else:
                            act.wait_ge(ft_full, upto(it, u, 8, 8))
                    src = wide[n % 4][:, 0:nf * P].rearrange("p (f v o) -> p f v o", f=nf, v=2)
                    dst = yt[:, :, 8 * n:8 * n + 2 * nf].rearrange("p o (f v) -> p f v o", v=2)
                    act.copy(dst, src).then_inc(fq_done, 1)

            def transposed(it, u, grp):
                for n in range(T2_FILLS):
                    k = grp * T2_FILLS + n
                    act.wait_ge(t2_full, upto(it, u, T2_ALL, k + 1))
                    if n == 0 and grp == 0:
                        act.wait_ge(tb_ready, upto(it, u, TB_ALL, TB_ALL))
                    elif n == 0:
                        act.wait_ge(in_full, upto(it, u, IN_ALL, IN_FILLS))
                    act.copy(qt[0][0:PX, :, :, 4 * n:4 * n + 4].rearrange("p t h o -> p o h t"),
                             ps[(n + 2) % 4][0:PX, :].rearrange("p (o h t) -> p o h t", o=4, h=2)).then_inc(t2_high, 1)

            def image(it, u, more):
                coefficients(it, u)
                if more:
                    rows_dft(it, u + 1)
                root(it, u, 1)
                normalised(it, u)
                if more:
                    spectrum(it, u + 1)
                pixels_and_spectra(it, u, 0, more)
                products(it, u, 0)
                pixels_and_spectra(it, u, 1, more)
                transposed(it, u, 0)
                products(it, u, 1)
                if more:
                    spectrum_normalised(it, u + 1)
                transposed(it, u, 1)
                if more:
                    mixed(it, u + 1)
                    high_parts(it, u + 1)

            act.dma_start(gmean[:, :], c_gmean).then_inc(const_in, 16)
            for dst, src in ((ident, c_ident), (dft, c_dft), (ident16, c_ident16),
                             (cols, c_cols), (w0, cw0), (w1, cw1), (wm, w_mix), (fwd, c_fwd), (inv, c_inv),
                             (brow, conv_b), (b1, bias)):
                act.dma_start(dst[:, :], src).then_inc(const_in, 16)
            act.dma_start(taps[:, :, :], c_taps.rearrange("p (a m) -> p a m", m=P)).then_inc(const_in, 16)
            act.dma_start(rows[:, :, :], c_rows.rearrange("p (a m) -> p a m", m=H)).then_inc(const_in, 16)
            act.wait_ge(pads_set, 1)
            root(0, 0, 0)
            rows_dft(0, 0)
            spectrum(0, 0)
            spectrum_normalised(0, 0)
            mixed(0, 0)
            high_parts(0, 0)
            act.wait_ge(weight_done, 4)
            trips(act, image)

        @block.tensor
        def _(pe):
            def mean(it, u, n, j):
                pe.wait_ge(stat_ready, upto(it, u, 4, 2 * n + j + 1))
                pe.matmul(ps[1 - j][:, 0:1], gmean[:, :], sm[n][:, 0:1] if j == 0 else sm[n][:, 3:4],
                          start=True, stop=True).then_inc(stat_mean, 1)

            def rows_dft(it, u, n):
                q, gq = n // 4, n % 4
                pe.wait_ge(xh_in[n % 4], upto(it, u, 16 * XH_CHUNKS // 4, 16 * (n // 4 + 1)))
                pe.matmul(wide[q][32 * gq:32 * gq + 32, :], dft[:, :], xh[n % 4][:, :, :].rearrange("p c w -> p (c w)"),
                          start=True, stop=True).then_inc(xh_read, 1)

            def rows_dft_transposed(it, u, quarters):
                for q in quarters:
                    pe.wait_ge(a_done, upto(it, u, 4, q + 1))
                    if q >= 2:
                        pe.wait_ge(b_done, upto(it, u, 4, q - 1))
                    for cc in range(4):
                        ins = pe.transpose(ps[2 + q % 2][:, P * cc:P * cc + P], a_t[:, q, P * cc:P * cc + P], ident[:, :])
                    ins.then_inc(b_full, 1)

            def columns_dft(it, u, part):
                if part[0] == 0:
                    pe.wait_ge(b_done, upto(it, u, 4, 4))
                for kx in part:
                    ins = pe.matmul(wide[0][:, 32 * kx:32 * kx + 32], b_t[:, 2 * kx:2 * kx + 2, :].rearrange("p k c -> p (k c)"),
                                    dft[:, :], start=True, stop=True)
                if part[-1] == TRUNC - 1:
                    ins.then_inc(uu_full, 1)

            def mix(it, u, groups):
                for q in groups:
                    if q == 0:
                        pe.wait_ge(uu_done, upto(it, u, 2, 2))
                    pe.matmul(wide[q][:, 0:2 * K0 * C], u_t[:, q, :, :].rearrange("p kx n -> p (kx n)"), wm[:, :],
                              start=True, stop=True).then_inc(y_full, 1)

            def sum_taps(it, u):
                pe.wait_ge(y_done, upto(it, u, 4, 4))
                for n in range(2 * K0):
                    ins = pe.matmul(wide[0][:, 0:4 * C].rearrange("p (q o) -> p q o", o=C), taps[:, n, :],
                                    y_t[:, :, C * n:C * n + C], start=(n == 0), stop=(n == 2 * K0 - 1))
                ins.then_inc(z_full, 1)

            def rows_inverse(it, u):
                pe.wait_ge(z_done, upto(it, u, 1, 1))
                for q in range(4):
                    for r in range(2):
                        ins = pe.matmul(wide[q][:, 4 * C * r:4 * C * r + 4 * C], rows[:, 2 * q + r, :], z_t,
                                        start=True, stop=True)
                    ins.then_inc(gg_full, 1)

            def coefficients(it, u):
                pe.wait_ge(dup_done, upto(it, u, 1, 1))
                for n in range(8):
                    if FT_BANKS[n] in FT_BANKS[:n]:
                        held = max(m for m in range(n) if FT_BANKS[m] == FT_BANKS[n])
                        pe.wait_ge(ft_odd if n % 2 else ft_even, upto(it, u, 4, held // 2 + 1))
                    bank = ps[FT_BANKS[n]][:, :].bitcast(f16)
                    for j in range(8):
                        ins = pe.transpose(bank[:, P * j:P * j + P], g16[:, 8 * n + j, :, :].rearrange("p v k -> p (v k)"),
                                           ident16[:, :])
                    ins.then_inc(ft_full, 1)

            def convolve(it, u, more):
                pe.wait_ge(g_used, upto(it, u, GCHUNKS, GCHUNKS))
                between = {2: range(0, 4), 6: range(4, 8), 10: range(8, 12), 14: range(12, 16)}
                quarters = {11: range(0, 1), 12: range(1, 2), 13: range(2, 3), 15: range(3, 4)}
                for n in range(CONV_FILLS):
                    h, j = n % 2, n // 2
                    r = 32 * h + 4 * j
                    if n >= 2:
                        pe.wait_ge(conv_done, upto(it, u, CONV_FILLS, n - 1))
                    bank = ps[n % 2]
                    pe.matmul(bank[:, :], w0[:, :], s[:, r:r + 4, :].rearrange("p r w -> p (r w)"), start=True, stop=False)
                    pe.matmul(bank[:, :], w1[:, :], s[:, r + 1:r + 5, :].rearrange("p r w -> p (r w)"), start=False, stop=False)
                    if n == 0:
                        pe.wait_ge(ft_even, upto(it, u, 4, 4))
                        pe.wait_ge(ft_odd, upto(it, u, 4, 4))
                    for i in range(4):
                        ins = pe.matmul(bank[:, W * i:W * i + W],
                                        ft[:, 2 * (r + i):2 * (r + i) + 2, :].rearrange("p par o -> p (par o)"),
                                        cols[:, :], start=False, stop=(i == 3))
                    ins.then_inc(conv_full, 1)
                    if more and n in between:
                        for m in between[n]:
                            rows_dft(it, u + 1, m)
                    if more and n in quarters:
                        rows_dft_transposed(it, u + 1, quarters[n])
                pe.wait_ge(conv_done, upto(it, u, CONV_FILLS, CONV_FILLS))

            def pixels_and_spectra(it, u, grp, more):
                for n in range(T1_FILLS + 1):
                    if more and grp and n == 2:
                        mean(it, u + 1, 0, 1)
                    if n < T1_FILLS:
                        k = grp * T1_FILLS + n
                        if k >= 2:
                            pe.wait_ge(t1_done, upto(it, u, T1_ALL, k - 1))
                        pe.wait_ge(tb_ready, upto(it, u, TB_ALL, k // 2 + 1))
                        for j in range(4):
                            tile = tb[(k // 2) % 2][:, PX * (4 * (k % 2) + j):PX * (4 * (k % 2) + j) + PX]
                            ins = pe.transpose(ps[2 + n % 2][0:PX, P * j:P * j + P], tile, ident[:, :])
                        ins.then_inc(t1_full, 1)
                    if n >= 1:
                        m = n - 1
                        k = grp * FW_FILLS + m // 2
                        if m % 2 == 0 and k >= 2:
                            for done in ((fw_odd_upper, fw_odd_lower) if k % 2 else (fw_even,)):
                                pe.wait_ge(done, upto(it, u, FW_ALL // 2, k // 2))
                        if m == 0 and grp == 1:
                            pe.wait_ge(fq_done, upto(it, u, FQ_ALL, FQ_FILLS))
                        pe.wait_ge(t1_done, upto(it, u, T1_ALL, grp * T1_FILLS + m + 1))
                        for j in range(4):
                            ins = pe.matmul(pw[(m // 2) % 2][:, m % 2, PX * j:PX * j + PX],
                                            px[m % 2][:, P * j:P * j + P], fwd[:, :], start=True, stop=True)
                        ins.then_inc(px_used, 1)

            def products(it, u, grp, inverses=False):
                for done in (fw_even, fw_odd_upper, fw_odd_lower):
                    pe.wait_ge(done, upto(it, u, FW_ALL // 2, (grp + 1) * FW_FILLS // 2))
                for n in range(FQ_FILLS):
                    k = grp * FQ_FILLS + n
                    if n >= 4:
                        pe.wait_ge(fq_done, upto(it, u, FQ_ALL, k - 3))
                    for j in range(min(4, SLOTS - 4 * n)):
                        ins = pe.matmul(wide[n % 4][:, P * j:P * j + P], spec[:, 4 * n + j, :], wf[:, 4 * n + j, :],
                                        start=True, stop=True)
                    ins.then_inc(fq_full, 1)
                    if inverses and n >= FQ_FILLS - IN_FILLS - 1:
                        m = n - (FQ_FILLS - IN_FILLS - 1)
                        if m == 0:
                            qt_written(it, u, 0)
                        if m < IN_FILLS:
                            inverse(it, u, 0, m)

            def transpose(it, u, grp, more):
                mixed_after = [4, 7, 10, 13]
                pe.wait_ge(fq_done, upto(it, u, FQ_ALL, (grp + 1) * FQ_FILLS))
                for n in range(T2_FILLS):
                    k = grp * T2_FILLS + n
                    if k >= 4:
                        pe.wait_ge(t2_low, upto(it, u, T2_ALL, k - 3))
                    if n == 2 and grp == 0 and more:
                        pe.wait_ge(v_ready, upto(it, u + 1, 2, 1))
                    if n == 2 and grp:
                        pe.wait_ge(in_done, upto(it, u, IN_ALL, IN_FILLS))
                    for j in range(4):
                        ins = pe.transpose(ps[(n + 2) % 4][0:PX, P * j:P * j + P], yt[:, 4 * n + j, :], ident[:, :])
                    ins.then_inc(t2_full, 1)
                    if more and grp and n in mixed_after:
                        if n == mixed_after[0]:
                            pe.wait_ge(fq_done, upto(it, u, FQ_ALL, FQ_ALL))
                        q = mixed_after.index(n)
                        mix(it, u + 1, range(q, q + 1))

            def qt_written(it, u, grp):
                pe.wait_ge(t2_low, upto(it, u, T2_ALL, (grp + 1) * T2_FILLS))

            def inverse(it, u, grp, n):
                k = grp * IN_FILLS + n
                if k >= 2:
                    pe.wait_ge(in_done, upto(it, u, IN_ALL, k - 1))
                for j in range(8):
                    t = 8 * n + j
                    for v, w in ((0, 0), (0, 1), (1, 0)):
                        ins = pe.matmul(ps[n % 2][:, KEPT * j:KEPT * j + KEPT],
                                        qt[v][0:PX, t, :, :].rearrange("p h o -> p (h o)"),
                                        inv[0:PX, KEPT * w:KEPT * w + KEPT], start=(v + w == 0), stop=(v == 1))
                ins.then_inc(in_full, 1)

            def image(it, u, more):
                coefficients(it, u)
                convolve(it, u, more)
                if more:
                    columns_dft(it, u + 1, range(0, 9))
                mean(it, u, 1, 0)
                if more:
                    columns_dft(it, u + 1, range(9, 13))
                mean(it, u, 1, 1)
                if more:
                    columns_dft(it, u + 1, range(13, TRUNC))
                pe.wait_ge(weight_done, 4)
                pixels_and_spectra(it, u, 0, more)
                products(it, u, 0)
                if more:
                    mean(it, u + 1, 0, 0)
                pixels_and_spectra(it, u, 1, more)
                transpose(it, u, 0, more)
                products(it, u, 1, True)
                transpose(it, u, 1, more)
                qt_written(it, u, 1)
                for n in range(IN_FILLS):
                    if more and n == 2:
                        sum_taps(it, u + 1)
                    if more and n == 4:
                        rows_inverse(it, u + 1)
                    inverse(it, u, 1, n)
                pe.wait_ge(in_done, upto(it, u, IN_ALL, IN_ALL))

            pe.wait_ge(const_in, 16 * 14)
            mean(0, 0, 0, 0)
            mean(0, 0, 0, 1)
            for n in range(XH_CHUNKS):
                rows_dft(0, 0, n)
            rows_dft_transposed(0, 0, range(4))
            columns_dft(0, 0, range(TRUNC))
            mix(0, 0, range(4))
            sum_taps(0, 0)
            rows_inverse(0, 0)
            trips(pe, image)


_OUT = "out_dram"


def kernel(x, L0_conv_conv_w, L0_conv_conv_b, L0_conv_bias, L1_conv_weight_re, L1_conv_weight_im):
    import numpy as _np
    import concourse.bacc as _bacc
    from concourse import mybir as _mybir
    from concourse.bass_utils import run_bass_kernel_spmd as _run

    x = _np.ascontiguousarray(x)
    cw = _np.asarray(L0_conv_conv_w).transpose(1, 2, 0)
    cw0 = _np.zeros((2, C, 2, C), _np.float32)
    cw1 = _np.zeros((2, C, 2, C), _np.float32)
    cw0[0, :, 0], cw0[1, :, 0], cw0[1, :, 1] = cw[:, 0], cw[:, 1], cw[:, 0]
    cw1[0, :, 0], cw1[0, :, 1], cw1[1, :, 1] = cw[:, 2], cw[:, 1], cw[:, 2]
    mix = _np.zeros((2, C, 2, K0, C), _np.float32)
    mix[0, :, 0], mix[1, :, 1] = cw, cw
    wre = _np.asarray(L1_conv_weight_re).transpose(1, 2, 3, 0)
    wim = _np.asarray(L1_conv_weight_im).transpose(1, 2, 3, 0)
    p_w = _np.zeros((2, C, SLOTS, 2, C), _np.float32)
    q_w = _np.zeros((2, C, SLOTS, 2, C), _np.float32)
    for n, (k, l, cplx) in enumerate(frequency_slots()):
        for lane, f in enumerate((k, l)):
            m = ((-f[0]) % N_FREQ, (-f[1]) % N_FREQ)
            p_w[lane, :, n, lane], q_w[lane, :, n, lane] = wre[:, f[0], f[1]], wre[:, m[0], m[1]]
            if cplx:
                a, b = wim[:, f[0], f[1]], wim[:, m[0], m[1]]
                p_w[lane, :, n, 1 - lane], q_w[lane, :, n, 1 - lane] = (a, b) if lane == 0 else (b, a)
    arrays = {
        "x": x, "p_w": p_w.reshape(P, SLOTS, P), "q_w": q_w.reshape(P, SLOTS, P), "cw0": cw0.reshape(P, P),
        "cw1": cw1.reshape(P, P), "w_mix": mix.reshape(P, 2 * K0 * C),
        "conv_b": _np.asarray(L0_conv_conv_b).reshape(1, C), "bias": _np.asarray(L0_conv_bias).reshape(1, 1),
    }
    tables = constants()
    for name in ("ident", "ident16", "gmean", "fwd", "inv", "dft", "taps", "rows", "cols"):
        arrays["c_" + name] = tables[name]
    nc = _bacc.Bacc("TRN2", target_bir_lowering=False, num_devices=1)
    args, given = [], {}
    for name, a in arrays.items():
        a = _np.ascontiguousarray(a)
        given[f"in_{name}_dram"] = a
        args.append(nc.dram_tensor(f"in_{name}_dram", a.shape, _mybir.dt.from_np(a.dtype), kind="ExternalInput").ap())
    args.append(nc.dram_tensor(_OUT, x.shape, _mybir.dt.float32, kind="ExternalOutput").ap())
    nc.disable_value_cache = True
    conv_preact_kernel(nc, *args)
    r = _run(nc, [given], core_ids=[0])
    return r.results[0][_OUT]
```
